# Optimizing a Trainium2 kernel written in Bass

```python
import numpy as np
import jax
import jax.numpy as jnp

def _softmax(x, axis=-1):
    return jax.nn.softmax(x, axis=axis)

def _gelu(x):
    return jax.nn.gelu(x, approximate=True)

def _silu(x):
    return jax.nn.silu(x)

def _sigmoid(x):
    return jax.nn.sigmoid(x)

def _layernorm(x, axis=-1, eps=1e-05):
    m = jnp.mean(x, axis=axis, keepdims=True)
    v = jnp.var(x, axis=axis, keepdims=True)
    return (x - m) / jnp.sqrt(v + eps)

def _scatter_add(tgt, idx, src, axis=0):
    return tgt.at[idx].add(src)

def _segment_sum(src, seg, n):
    return jax.ops.segment_sum(src, seg, n)
kernel_name = 'mk_cond_resid_d2_seqx_r8_7495af'

def setup_inputs(seed: int=0):
    np.random.seed(seed)
    _w = jnp.asarray

    def _rec_inputs():
        import jax
        import jax.numpy as jnp
        _rk = jax.random.key(seed)
        x = -1.394e-06 + 0.9999 * jax.random.normal(jax.random.fold_in(_rk, 1), (32, 32, 256), jnp.float32)
        _lenS = 32 - jax.random.randint(jax.random.fold_in(_rk, 7), (32,), 0, max(1, 32 // 4) + 1, jnp.int32)
        _lenS2 = 32 - jax.random.randint(jax.random.fold_in(_rk, 8), (32,), 0, max(1, 32 // 4) + 1, jnp.int32)
        cond_2048 = -0.00499425 + 1.0058 * jax.random.normal(jax.random.fold_in(_rk, 11), (32, 256), jnp.float32)
        return (x, cond_2048)
    x, cond_2048 = _rec_inputs()

    def _L0_cond_setup():
        import jax, jax.numpy as jnp
        import numpy as np
        B, T, D = (16, 128, 256)
        key = jax.random.key(seed)
        k0, k1, k2, k3 = jax.random.split(key, 4)
        scale = 1.0 / np.sqrt(D)
        return {'initial_state': jax.random.normal(k0, (B, D), jnp.float32), 'inputs': jax.random.normal(k1, (B, T, D), jnp.float32), 'W_ih': jax.random.normal(k2, (D, 3 * D), jnp.float32) * scale, 'W_hh': jax.random.normal(k3, (D, 3 * D), jnp.float32) * scale, 'b_ih': jnp.zeros((3 * D,), jnp.float32), 'b_hh': jnp.zeros((3 * D,), jnp.float32)}
    _L0_cond_all = _L0_cond_setup()
    _L0_cond_in = {k: v for k, v in _L0_cond_all.items() if k in ('W_ih', 'W_hh', 'b_ih', 'b_hh')}
    del _L0_cond_all

    def _L1_cond_setup():
        import jax, jax.numpy as jnp
        import numpy as np
        DT = 0.01
        EPSILON = 0.08
        ALPHA = 0.7
        BETA = 0.8
        CLAMP = 20.0
        B, T, N = (32, 128, 256)

        def _derivative(q, p, drive, coupling, bias):
            i_couple = jnp.tanh(q) @ coupling.T
            dq = q - q ** 3 / 3.0 - p + drive + i_couple + bias
            dp = EPSILON * (q + ALPHA - BETA * p)
            return (dq, dp)

        def _rk4_step(q, p, drive, coupling, bias):
            dq1, dp1 = _derivative(q, p, drive, coupling, bias)
            dq2, dp2 = _derivative(q + 0.5 * DT * dq1, p + 0.5 * DT * dp1, drive, coupling, bias)
            dq3, dp3 = _derivative(q + 0.5 * DT * dq2, p + 0.5 * DT * dp2, drive, coupling, bias)
            dq4, dp4 = _derivative(q + DT * dq3, p + DT * dp3, drive, coupling, bias)
            q_next = q + DT / 6.0 * (dq1 + 2 * dq2 + 2 * dq3 + dq4)
            p_next = p + DT / 6.0 * (dp1 + 2 * dp2 + 2 * dp3 + dp4)
            q_next = jnp.clip(q_next, -CLAMP, CLAMP)
            p_next = jnp.clip(p_next, -CLAMP, CLAMP)
            return (q_next, p_next)
        key = jax.random.key(seed)
        k1, k2, k3, k4 = jax.random.split(key, 4)
        return {'q0': jax.random.normal(k1, (B, N), dtype=jnp.float32), 'p0': jax.random.normal(k2, (B, N), dtype=jnp.float32), 'input_drive_seq': jax.random.normal(k3, (B, T, N), dtype=jnp.float32), 'coupling': jax.random.normal(k4, (N, N), dtype=jnp.float32) * 0.01, 'bias': jnp.zeros((N,), dtype=jnp.float32)}
    _L1_cond_all = _L1_cond_setup()
    _L1_cond_in = {k: v for k, v in _L1_cond_all.items() if k in ('coupling', 'bias')}
    del _L1_cond_all
    return {'x': x, 'cond_2048': cond_2048, 'L0_cond_W_ih': _L0_cond_in['W_ih'], 'L0_cond_W_hh': _L0_cond_in['W_hh'], 'L0_cond_b_ih': _L0_cond_in['b_ih'], 'L0_cond_b_hh': _L0_cond_in['b_hh'], 'L1_cond_coupling': _L1_cond_in['coupling'], 'L1_cond_bias': _L1_cond_in['bias']}

def reference(x, cond_2048, L0_cond_W_ih, L0_cond_W_hh, L0_cond_b_ih, L0_cond_b_hh, L1_cond_coupling, L1_cond_bias):
    import jax
    import jax.numpy as jnp

    def _L0_cond_ref(initial_state, inputs, W_ih, W_hh, b_ih, b_hh):
        import jax, jax.numpy as jnp
        import numpy as np
        B, T, D = (16, 128, 256)
        "ScanOverTime(GRU cell): sequential per-timestep module call with\n            dict-state passing; merge_dict_trees stacks the per-step\n            'state_predicted' tensors along axis=1 -> [B, T, D]."

        def cell(h, x):
            gi = x @ W_ih + b_ih
            gh = h @ W_hh + b_hh
            i_r, i_z, i_n = jnp.split(gi, 3, axis=-1)
            h_r, h_z, h_n = jnp.split(gh, 3, axis=-1)
            r = jax.nn.sigmoid(i_r + h_r)
            z = jax.nn.sigmoid(i_z + h_z)
            n = jnp.tanh(i_n + r * h_n)
            h_new = (1.0 - z) * n + z * h
            return (h_new, h_new)
        xs = jnp.swapaxes(inputs, 0, 1)
        _, hs = jax.lax.scan(cell, initial_state, xs)
        return jnp.swapaxes(hs, 0, 1)

    def _L1_cond_ref(q0, p0, input_drive_seq, coupling, bias):
        import jax, jax.numpy as jnp
        import numpy as np
        DT = 0.01
        EPSILON = 0.08
        ALPHA = 0.7
        BETA = 0.8
        CLAMP = 20.0
        B, T, N = (32, 128, 256)

        def _derivative(q, p, drive, coupling, bias):
            i_couple = jnp.tanh(q) @ coupling.T
            dq = q - q ** 3 / 3.0 - p + drive + i_couple + bias
            dp = EPSILON * (q + ALPHA - BETA * p)
            return (dq, dp)

        def _rk4_step(q, p, drive, coupling, bias):
            dq1, dp1 = _derivative(q, p, drive, coupling, bias)
            dq2, dp2 = _derivative(q + 0.5 * DT * dq1, p + 0.5 * DT * dp1, drive, coupling, bias)
            dq3, dp3 = _derivative(q + 0.5 * DT * dq2, p + 0.5 * DT * dp2, drive, coupling, bias)
            dq4, dp4 = _derivative(q + DT * dq3, p + DT * dp3, drive, coupling, bias)
            q_next = q + DT / 6.0 * (dq1 + 2 * dq2 + 2 * dq3 + dq4)
            p_next = p + DT / 6.0 * (dp1 + 2 * dp2 + 2 * dp3 + dp4)
            q_next = jnp.clip(q_next, -CLAMP, CLAMP)
            p_next = jnp.clip(p_next, -CLAMP, CLAMP)
            return (q_next, p_next)
        drive_tbn = jnp.swapaxes(input_drive_seq, 0, 1)

        def scan_fn(carry, drive):
            q, p = carry
            q, p = _rk4_step(q, p, drive, coupling, bias)
            return ((q, p), q)
        (_, _), q_trace_tbn = jax.lax.scan(scan_fn, (q0, p0), drive_tbn)
        return jnp.swapaxes(q_trace_tbn, 0, 1)
    x = x + _L0_cond_ref(cond_2048, x, L0_cond_W_ih, L0_cond_W_hh, L0_cond_b_ih, L0_cond_b_hh)
    x = x + _L1_cond_ref(cond_2048, cond_2048, x, L1_cond_coupling, L1_cond_bias)
    return x

_drawn_inputs = setup_inputs


def setup_inputs(seed=0):
    import zlib

    import numpy as np

    out = dict(_drawn_inputs(seed))
    spreads = {'L0_cond_b_ih': (0.0, 0.1), 'L0_cond_b_hh': (0.0, 0.283), 'L1_cond_bias': (0.0, 0.572)}
    factors = {'L1_cond_coupling': 4.216}
    for name, (base, spread) in spreads.items():
        noise = np.random.default_rng([zlib.crc32(name.encode()), seed]).standard_normal(out[name].shape)
        drawn = base * np.exp(spread * noise) if base else spread * noise
        out[name] = jnp.asarray(drawn.astype(out[name].dtype))
    for name, factor in factors.items():
        out[name] = (out[name] * factor).astype(out[name].dtype)
    return out
```

```python
from contextlib import ExitStack

import concourse.bass as bass
from concourse import mybir


P = 128
B = 32
HALVES = 2
W = HALVES * B
GATES = 3
WSCALE = 256.0

DT = 0.01
HALF = 0.5 * DT
EPS = 0.08
ALPHA = 0.7
BETA = 0.8
CLAMP = 20.0
X = HALF * EPS * BETA

GAM = DT * EPS / 6.0
PE_ = 1 + 2 * (1 - X) + 2 * (1 - X + X * X) + (1 - 2 * X + 2 * X**2 - 2 * X**3)
P_OF_P0 = 1.0 - GAM * PE_ * BETA
P_CONST = GAM * PE_ * ALPHA
P_OF_Q = [GAM * (1 - 2 * X + 2 * X**2 - 2 * X**3), GAM * (2 - 2 * X + 2 * X**2), GAM * (2 - 2 * X), GAM]

STEP = [HALF, HALF, DT, DT / 6.0]
BASE_OF_E = [0.0, -HALF * HALF * EPS, -DT * HALF * EPS * (1 - X), -DT * DT * EPS / 6 * (1 - X + X * X)]
BASE_OF_P0 = [-STEP[s] - BETA * BASE_OF_E[s] for s in range(4)]
BASE_CONST = [ALPHA * BASE_OF_E[s] for s in range(4)]
BASE_OF_Q = [
    [],
    [1 - HALF * HALF * EPS],
    [1 + DT * HALF * EPS * X, -DT * HALF * EPS],
    [-1 / 3 - DT * DT * EPS / 6 * X * X, 1 / 3 + DT * DT * EPS / 6 * X, 2 / 3 - DT * DT * EPS / 6],
]
SELF = [1 + HALF, HALF, DT, 1 / 3 + DT / 6]


def build(nc, x_in, cond_in, wih_in, whh_in, bih_in, bhh_in, coup_in, fbias_in, out):
    f32 = mybir.dt.float32
    f16 = mybir.dt.float16
    ALU = mybir.AluOpType
    ACT = mybir.ActivationFunctionType
    T = x_in.shape[1]
    N3 = wih_in.shape[2]
    ND = coup_in.shape[2]

    ctx = ExitStack()
    with ctx:

        def sb(name, shape, dt=f32):
            return ctx.enter_context(nc.sbuf_tensor(name, shape, dt))

        def pb(name):
            return ctx.enter_context(nc.psum_tensor(name, [P, 512], f32))

        def sem(name):
            return ctx.enter_context(nc.semaphore(name))

        x = sb("x", [P, T * W])
        xb = sb("xb", [P, T * W])
        xhl = sb("xhl", [P, T * 2 * W], f16)
        outb = sb("outb", [P, T * W])
        wih = sb("wih", [P, 2, N3])
        whh = sb("whh", [P, 2, N3])
        coup = sb("coup", [P, 2, ND])
        fbias = sb("fbias", [P, 2])
        brow = sb("brow", [P, N3])
        wih1, wih2 = sb("wih1", [P, 2, N3], f16), sb("wih2", [P, 2, N3], f16)
        whh1, whh2 = sb("whh1", [P, 2, N3], f16), sb("whh2", [P, 2, N3], f16)
        cp1, cp2 = sb("cp1", [P, 2, ND], f16), sb("cp2", [P, 2, ND], f16)
        bsp = sb("bsp", [P, N3], f16)
        pick_both, pick_ih, pick_hh = sb("pick_both", [P, B], f16), sb("pick_ih", [P, B], f16), sb("pick_hh", [P, B], f16)

        h, h1, h2 = sb("h", [P, W]), sb("h1", [P, W], f16), sb("h2", [P, W], f16)
        tr, tz, z, n = sb("tr", [P, W]), sb("tz", [P, W]), sb("z", [P, W]), sb("n", [P, W])
        rh, npre, dhn, zd = sb("rh", [P, W]), sb("npre", [P, W]), sb("dhn", [P, W]), sb("zd", [P, W])
        drive = sb("drive", [P, W])

        qraw = sb("qraw", [P, W])
        q = [sb(f"q{s}", [P, W]) for s in range(4)]
        p0, praw = sb("p0", [P, W]), sb("praw", [P, W])
        t32, t1, t2 = sb("t32", [P, W]), sb("t1", [P, W], f16), sb("t2", [P, W], f16)
        sq, cub, rest = sb("sq", [P, W]), sb("cub", [P, W]), sb("rest", [P, W])
        sdrive = [sb(f"sdrive{s}", [P, W]) for s in range(4)]
        sp0 = [sb(f"sp0_{s}", [P, W]) for s in range(4)]
        base = [[sb(f"base{s}_{r}", [P, W]) for r in range(s + 1)] for s in range(4)]
        base0p = sb("base0p", [P, W])
        pq = [sb(f"pq{r}", [P, W]) for r in range(3)]
        pacc0 = sb("pacc0", [P, W])
        pacc = [sb(f"pacc_{r}", [P, W]) for r in range(3)]

        ps_c, ps_r, ps_z, ps_h, ps_i = pb("ps_c"), pb("ps_r"), pb("ps_z"), pb("ps_h"), pb("ps_i")

        ld_x, ld_wih, ld_whh, ld_coup, ld_b, ld_state, ld_fb = (sem(k) for k in (
            "ld_x", "ld_wih", "ld_whh", "ld_coup", "ld_b", "ld_state", "ld_fb"))
        brow_zero, picks, picks0 = sem("brow_zero"), sem("picks"), sem("picks0")
        hi_x, hi_wih, hi_whh, hi_coup, hi_b, hi_h = (sem(k) for k in ("hi_x", "hi_wih", "hi_whh", "hi_coup", "hi_b", "hi_h"))
        lo_x, lo_wih, lo_whh, lo_coup, lo_b, lo_h = (sem(k) for k in ("lo_x", "lo_wih", "lo_whh", "lo_coup", "lo_b", "lo_h"))
        xb_ready = sem("xb_ready")
        g_rz, g_h, g_r, g_rh, g_np, g_n, g_d, g_z, g_zd, g_hn, g_h1, g_dr = (
            sem("g0_" + k) for k in ("rz", "h", "r", "rh", "np", "n", "d", "z", "zd", "hn", "h1", "dr"))
        rh_ready, h2_ready, qraw_ready, p0_ready, x1_ready, base0p_ready = (
            sem(k) for k in ("rh_ready", "h2_ready", "qraw_ready", "p0_ready", "x1_ready", "base0p_ready"))
        sdrive_ready = sem("sdrive_ready")
        tr_ready, z_ready, tz_ready, zs_ready, m_ready, npre_ready, n_ready, dhn_ready, zd_ready, h_ready = (
            sem(k) for k in ("tr_ready", "z_ready", "tz_ready", "zs_ready", "m_ready", "npre_ready", "n_ready", "dhn_ready",
                             "zd_ready", "h_ready"))
        h1_ready, drive_ready, sdrive0_ready = sem("h1_ready"), sem("drive_ready"), sem("sdrive0_ready")
        q_ready = [sem(f"q_ready{s}") for s in range(4)]
        t1_ready = [sem(f"t1_ready{s}") for s in range(4)]
        t32_ready = [sem(f"t32_ready{s}") for s in range(4)]
        t2_ready = [sem(f"t2_ready{s}") for s in range(4)]
        c_ready = [sem(f"c_ready{s}") for s in range(4)]
        sq_ready = [sem(f"sq_ready{s}") for s in range(4)]
        cub_ready = [sem(f"cub_ready{s}") for s in range(4)]
        rest_ready = [sem(f"rest_ready{s}") for s in range(4)]
        sp0_ready = sem("sp0_ready")
        base_ready = [[sem(f"base_ready{s}_{r}") for r in range(s + 1)] for s in range(4)]
        pq_ready = [sem(f"pq_ready{r}") for r in range(3)]
        pacc_ready = [sem(f"pacc_ready{r}") for r in range(3)]
        praw_ready = sem("praw_ready")
        out_ready, stored = sem("out_ready"), sem("stored")

        def wait(eng, s, value):
            if not isinstance(value, int) or value > 0:
                eng.wait_ge(s, value)

        def at(t, width):
            return bass.ds(t * width, width)

        def loop(eng, body):
            body(1)
            with eng.Fori(2, T - 1) as i:
                body(i)
            body(T - 1, last_gru=True)
            body(T, last=True)

        block = ctx.enter_context(nc.Block())

        @block.sync
        def _(sp):
            for t in (h, qraw, p0):
                sp.dma_start(t[:, :], cond_in).then_inc(ld_state, 16)
            sp.dma_start(wih[:, :, :], wih_in).then_inc(ld_wih, 16)
            sp.dma_start(x[:, :], x_in.rearrange("p t w -> p (t w)")).then_inc(ld_x, 16)
            sp.dma_start(coup[:, :, :], coup_in).then_inc(ld_coup, 16)

            def body(k):
                sp.wait_ge(out_ready, k)
                sp.dma_start(out[bass.ds(k - 1, 1), :, :].rearrange("o p w -> p (o w)"), outb[:, at(k - 1, W)]).then_inc(stored, 16)

            with sp.Fori(1, T + 1) as k:
                body(k)
            sp.wait_ge(stored, 16 * T)

        @block.gpsimd
        def _(pool):
            pool.memset(brow[:, :], 0.0).then_inc(brow_zero, 1)
            pool.memset(pick_both[:, :], 1.0).then_inc(picks, 1)
            pool.memset(pick_ih[:, :], 0.0).then_inc(picks0, 1)
            pool.memset(pick_hh[:, :], 0.0).then_inc(picks0, 1)
            pool.wait_ge(picks0, 2)
            for r in (0, 64):
                pool.memset(pick_ih[r : r + 32, :], 1.0).then_inc(picks, 1)
                pool.memset(pick_hh[r + 32 : r + 64, :], 1.0).then_inc(picks, 1)
            pool.wait_ge(picks, 5)
            pool.wait_ge(ld_x, 16)
            pool.wait_ge(ld_fb, 16)
            xv = x[:, :].rearrange("p (t k b) -> p t k b", k=HALVES, b=B)
            xbv = xb[:, :].rearrange("p (t k b) -> p t k b", k=HALVES, b=B)
            for k in range(HALVES):
                pool.tensor_scalar(xbv[:, :, k, :], xv[:, :, k, :], fbias[:, k : k + 1], None, ALU.add).then_inc(xb_ready, 1)
            pool.wait_ge(g_n, 1)
            pool.tensor_tensor(dhn[:, :], h[:, :], n[:, :], ALU.subtract).then_inc(g_d, 1)
            pool.wait_ge(g_d, 1)
            pool.wait_ge(g_z, 1)
            pool.tensor_tensor(zd[:, :], z[:, :], dhn[:, :], ALU.mult).then_inc(g_zd, 1)
            pool.wait_ge(g_zd, 1)
            pool.tensor_tensor(h[:, :], n[:, :], zd[:, :], ALU.add).then_inc(g_hn, 1)
            pool.wait_ge(g_hn, 1)
            pool.wait_ge(xb_ready, 2)
            pool.tensor_tensor(drive[:, :], xb[:, 0:W], h[:, :], ALU.add).then_inc(g_dr, 1)
            pool.wait_ge(g_h1, 1)
            pool.tensor_tensor(h2[:, :], h[:, :], h1[:, :], ALU.subtract).then_inc(h2_ready, 1)

            def body(i, last_gru=False, last=False):
                first = isinstance(i, int) and i == 1
                pool.wait_ge(sp0_ready, i)
                for s in range(1, 4):
                    pool.tensor_tensor(base[s][0][:, :], sp0[s][:, :], sdrive[s][:, :], ALU.add).then_inc(base_ready[s][0], 1)
                pool.wait_ge(pq_ready[0], i)
                pool.tensor_tensor(outb[:, at(i - 1, W)], x[:, at(i - 1, W)], h[:, :], ALU.add).then_inc(x1_ready, 1)
                if not first:
                    prev = outb[:, at(i - 2, W)]
                    pool.wait_ge(x1_ready, i - 1)
                    pool.tensor_tensor(prev, prev, q[0][:, :], ALU.add).then_inc(out_ready, 1)
                if not last:
                    pool.tensor_tensor(pacc[0][:, :], pacc0[:, :], pq[0][:, :], ALU.add).then_inc(pacc_ready[0], 1)
                    pool.wait_ge(pacc_ready[0], i)
                    pool.wait_ge(pq_ready[1], i)
                    pool.tensor_tensor(pacc[1][:, :], pacc[0][:, :], pq[1][:, :], ALU.add).then_inc(pacc_ready[1], 1)
                    pool.wait_ge(n_ready, i)
                    pool.tensor_tensor(dhn[:, :], h[:, :], n[:, :], ALU.subtract).then_inc(dhn_ready, 1)
                    pool.wait_ge(dhn_ready, i)
                    pool.tensor_tensor(zd[:, :], z[:, :], dhn[:, :], ALU.mult).then_inc(zd_ready, 1)
                    pool.wait_ge(zd_ready, i)
                    pool.tensor_tensor(h[:, :], n[:, :], zd[:, :], ALU.add).then_inc(h_ready, 1)
                    pool.wait_ge(h_ready, i)
                    pool.tensor_tensor(drive[:, :], xb[:, at(i, W)], h[:, :], ALU.add).then_inc(drive_ready, 1)
                    if not last_gru:
                        pool.wait_ge(h1_ready, i)
                        pool.tensor_tensor(h2[:, :], h[:, :], h1[:, :], ALU.subtract).then_inc(h2_ready, 1)
                    pool.wait_ge(pacc_ready[1], i)
                    pool.wait_ge(pq_ready[2], i)
                    pool.tensor_tensor(pacc[2][:, :], pacc[1][:, :], pq[2][:, :], ALU.add).then_inc(pacc_ready[2], 1)

            loop(pool, body)
            pool.wait_ge(q_ready[0], T + 1)
            pool.wait_ge(x1_ready, T)
            pool.tensor_tensor(outb[:, at(T - 1, W)], outb[:, at(T - 1, W)], q[0][:, :], ALU.add).then_inc(out_ready, 1)

        @block.tensor
        def _(pe):
            r_cols, z_cols, n_cols = 0, HALVES, 2 * HALVES

            def mm(ps, half, w, k, tile, mov, start):
                return pe.matmul(ps[:, half * B : (half + 1) * B], w[:, k, tile * P : (tile + 1) * P], mov,
                                 start=start, stop=True, skip_group_check=True)

            def x_part(ps, first_tile, t, pick):
                for half in range(HALVES):
                    tile = first_tile + half
                    pe.matmul(ps[:, half * B : (half + 1) * B], bsp[:, tile * P : (tile + 1) * P], pick[:, :],
                              start=half == 0, stop=True, skip_group_check=True)
                    for k in range(2):
                        xk = [xhl[:, bass.ds(t * 2 * W + part * W + k * B, B)] for part in range(2)]
                        mm(ps, half, wih1, k, tile, xk[0], False)
                        mm(ps, half, wih2, k, tile, xk[0], False)
                        last = mm(ps, half, wih1, k, tile, xk[1], False)
                return last

            def hn_bias():
                for half in range(HALVES):
                    tile = n_cols + half
                    last = pe.matmul(ps_h[:, half * B : (half + 1) * B], bsp[:, tile * P : (tile + 1) * P], pick_hh[:, :],
                                     start=half == 0, stop=True, skip_group_check=True)
                return last

            def h_part(ps, first_tile):
                for half in range(HALVES):
                    tile = first_tile + half
                    for k in range(2):
                        mm(ps, half, whh1, k, tile, h1[:, k * B : (k + 1) * B], False)
                        mm(ps, half, whh2, k, tile, h1[:, k * B : (k + 1) * B], False)
                        last = mm(ps, half, whh1, k, tile, h2[:, k * B : (k + 1) * B], False)
                return last

            pe.wait_ge(picks, 5)
            pe.wait_ge(lo_b, 1)
            pe.wait_ge(lo_x, 1)
            pe.wait_ge(lo_wih, 1)
            x_part(ps_r, r_cols, 0, pick_both)
            x_part(ps_i, n_cols, 0, pick_ih)
            x_part(ps_z, z_cols, 0, pick_both)
            hn_bias()
            pe.wait_ge(lo_whh, 1)
            pe.wait_ge(lo_h, 1)
            h_part(ps_r, r_cols)
            h_part(ps_z, z_cols).then_inc(g_rz, 1)
            h_part(ps_h, n_cols).then_inc(g_h, 1)
            pe.wait_ge(g_z, 1)
            x_part(ps_r, r_cols, 1, pick_both)
            x_part(ps_z, z_cols, 1, pick_both)
            pe.wait_ge(g_np, 1)
            x_part(ps_i, n_cols, 1, pick_ih)
            hn_bias()
            pe.wait_ge(h2_ready, 1)
            h_part(ps_r, r_cols)
            h_part(ps_h, n_cols).then_inc(rh_ready, 1)

            def coupling_hi():
                for half in range(HALVES):
                    for k in range(2):
                        tk = t1[:, k * B : (k + 1) * B]
                        mm(ps_c, half, cp1, k, half, tk, half == 0 and k == 0)
                        mm(ps_c, half, cp2, k, half, tk, False)

            def coupling_lo():
                for half in range(HALVES):
                    for k in range(2):
                        last = mm(ps_c, half, cp1, k, half, t2[:, k * B : (k + 1) * B], False)
                return last

            pe.wait_ge(lo_coup, 1)

            def body(i, last_gru=False, last=False):
                for s in range(4):
                    pe.wait_ge(t1_ready[s], i)
                    coupling_hi()
                    pe.wait_ge(t2_ready[s], i)
                    coupling_lo().then_inc(c_ready[s], 1)
                    if last:
                        continue
                    if s == 0:
                        h_part(ps_z, z_cols).then_inc(z_ready, 1)
                        if not last_gru:
                            pe.wait_ge(tr_ready, i)
                            x_part(ps_r, r_cols, i + 1, pick_both)
                    if s == 2 and not last_gru:
                        pe.wait_ge(npre_ready, i)
                        pe.wait_ge(tz_ready, i)
                        x_part(ps_i, n_cols, i + 1, pick_ih)
                        x_part(ps_z, z_cols, i + 1, pick_both)
                        hn_bias()
                    if s == 3 and not last_gru:
                        pe.wait_ge(h2_ready, i + 1)
                        h_part(ps_r, r_cols)
                        h_part(ps_h, n_cols).then_inc(rh_ready, 1)

            loop(pe, body)

        @block.scalar
        def _(act):
            act.dma_start(whh[:, :, :], whh_in).then_inc(ld_whh, 16)
            act.dma_start(fbias[:, :], fbias_in).then_inc(ld_fb, 16)
            act.wait_ge(brow_zero, 1)
            for r in (0, 64):
                act.dma_start(brow[r : r + 1, :], bih_in).then_inc(ld_b, 16)
                act.dma_start(brow[r + 32 : r + 33, :], bhh_in).then_inc(ld_b, 16)

            def affine(out_, in_, scale, shift=0.0):
                return act.activation(out_, in_, ACT.Copy, scale=scale, bias=shift)

            act.wait_ge(ld_state, 48)
            affine(h1[:, :], h[:, :], 1.0).then_inc(hi_h, 1)
            act.wait_ge(ld_b, 64)
            affine(bsp[:, :], brow[:, :], WSCALE).then_inc(hi_b, 1)
            act.wait_ge(ld_wih, 16)
            affine(wih1[:, :, :], wih[:, :, :], WSCALE).then_inc(hi_wih, 1)
            act.wait_ge(ld_x, 16)
            xv = x[:, :].rearrange("p (t w) -> p t w", w=W)
            xhlv = xhl[:, :].rearrange("p (t a w) -> p t a w", a=2, w=W)
            affine(xhlv[:, :, 0, :], xv, 1.0).then_inc(hi_x, 1)
            act.wait_ge(ld_whh, 16)
            affine(whh1[:, :, :], whh[:, :, :], WSCALE).then_inc(hi_whh, 1)
            act.wait_ge(ld_coup, 16)
            affine(cp1[:, :, :], coup[:, :, :], WSCALE).then_inc(hi_coup, 1)

            act.wait_ge(g_rz, 1)
            act.activation(tr[:, :], ps_r[:, 0:W], ACT.Tanh, scale=0.5 / WSCALE).then_inc(g_r, 1)
            act.activation(tz[:, :], ps_z[:, 0:W], ACT.Tanh, scale=0.5 / WSCALE).then_inc(g_r, 1)
            act.wait_ge(g_r, 2)
            affine(z[:, :], tz[:, :], 0.5, 0.5).then_inc(g_z, 1)
            act.wait_ge(g_np, 1)
            act.activation(n[:, :], npre[:, :], ACT.Tanh, scale=1.0 / WSCALE).then_inc(g_n, 1)
            act.wait_ge(g_hn, 1)
            affine(h1[:, :], h[:, :], 1.0).then_inc(g_h1, 1)
            act.wait_ge(g_dr, 1)
            for s in range(4):
                affine(sdrive[s][:, :], drive[:, :], STEP[s], BASE_CONST[s]).then_inc(sdrive_ready, 1)

            def body(i, last_gru=False, last=False):
                for s in range(4):
                    qs = qraw if s == 0 else q[s]
                    act.wait_ge(qraw_ready if s == 0 else q_ready[s], i)
                    act.activation(t1[:, :], qs[:, :], ACT.Tanh).then_inc(t1_ready[s], 1)
                    act.activation(t32[:, :], qs[:, :], ACT.Tanh).then_inc(t32_ready[s], 1)
                    if s == 0:
                        act.wait_ge(p0_ready, i)
                        for r in range(1, 4):
                            ins = affine(sp0[r][:, :], p0[:, :], BASE_OF_P0[r])
                        ins.then_inc(sp0_ready, 1)
                        if not last:
                            affine(pacc0[:, :], p0[:, :], P_OF_P0, P_CONST)
                        act.wait_ge(q_ready[0], i)
                        affine(pq[0][:, :], q[0][:, :], P_OF_Q[0]).then_inc(pq_ready[0], 1)
                        if not last:
                            act.wait_ge(rh_ready, i)
                            act.activation(tr[:, :], ps_r[:, 0:W], ACT.Tanh, scale=0.5 / WSCALE).then_inc(tr_ready, 1)
                    if last:
                        continue
                    if s == 1:
                        affine(pq[1][:, :], q[1][:, :], P_OF_Q[1]).then_inc(pq_ready[1], 1)
                        act.wait_ge(z_ready, i)
                        act.activation(tz[:, :], ps_z[:, 0:W], ACT.Tanh, scale=0.5 / WSCALE).then_inc(tz_ready, 1)
                        act.wait_ge(tz_ready, i)
                        affine(z[:, :], tz[:, :], 0.5, 0.5).then_inc(zs_ready, 1)
                        act.wait_ge(npre_ready, i)
                        act.activation(n[:, :], npre[:, :], ACT.Tanh, scale=1.0 / WSCALE).then_inc(n_ready, 1)
                    if s == 2:
                        affine(pq[2][:, :], q[2][:, :], P_OF_Q[2]).then_inc(pq_ready[2], 1)
                        if not last_gru:
                            act.wait_ge(h_ready, i)
                            affine(h1[:, :], h[:, :], 1.0).then_inc(h1_ready, 1)
                    if s == 3:
                        act.wait_ge(drive_ready, i)
                        affine(sdrive[0][:, :], drive[:, :], STEP[0], BASE_CONST[0]).then_inc(sdrive0_ready, 1)
                        for r in range(1, 4):
                            affine(sdrive[r][:, :], drive[:, :], STEP[r], BASE_CONST[r])

            loop(act, body)

        @block.vector
        def _(dve):
            def stt(out_, in0, scalar, in1, op0=ALU.mult, op1=ALU.add):
                return dve.scalar_tensor_tensor(out_, in0, scalar, in1, op0, op1)

            def clip(out_, in_):
                return dve.tensor_scalar(out_, in_, CLAMP, -CLAMP, ALU.min, ALU.max)

            def base_of_p0():
                return stt(base0p[:, :], p0[:, :], BASE_OF_P0[0], sdrive[0][:, :])

            dve.wait_ge(hi_h, 1)
            dve.tensor_tensor(h2[:, :], h[:, :], h1[:, :], ALU.subtract).then_inc(lo_h, 1)
            dve.wait_ge(hi_b, 1)
            stt(bsp[64:128, :], brow[64:128, :], WSCALE, bsp[64:128, :], op1=ALU.subtract).then_inc(lo_b, 1)
            dve.wait_ge(hi_wih, 1)
            stt(wih2[:, :, :], wih[:, :, :], WSCALE, wih1[:, :, :], op1=ALU.subtract).then_inc(lo_wih, 1)
            dve.wait_ge(hi_x, 1)
            xv = x[:, :].rearrange("p (t w) -> p t w", w=W)
            xhlv = xhl[:, :].rearrange("p (t a w) -> p t a w", a=2, w=W)
            dve.tensor_tensor(xhlv[:, :, 1, :], xv, xhlv[:, :, 0, :], ALU.subtract).then_inc(lo_x, 1)
            dve.wait_ge(hi_whh, 1)
            stt(whh2[:, :, :], whh[:, :, :], WSCALE, whh1[:, :, :], op1=ALU.subtract).then_inc(lo_whh, 1)
            dve.wait_ge(hi_coup, 1)
            stt(cp2[:, :, :], coup[:, :, :], WSCALE, cp1[:, :, :], op1=ALU.subtract).then_inc(lo_coup, 1)

            dve.wait_ge(g_h, 1)
            dve.wait_ge(g_r, 2)
            stt(rh[:, :], tr[:, :], 1.0, ps_h[:, 0:W], ALU.add, ALU.mult).then_inc(g_rh, 1)
            dve.wait_ge(g_rh, 1)
            stt(npre[:, :], rh[:, :], 0.5, ps_i[:, 0:W]).then_inc(g_np, 1)
            dve.wait_ge(ld_state, 48)
            dve.tensor_copy(q[0][:, :], qraw[:, :]).then_inc(qraw_ready, 1)
            dve.tensor_copy(praw[:, :], p0[:, :]).then_inc(p0_ready, 1)
            dve.wait_ge(sdrive_ready, 4)
            base_of_p0().then_inc(base0p_ready, 1)

            def base_term(s, r, i):
                dve.wait_ge(base_ready[s][r], i)
                return stt(base[s][r + 1][:, :], q[r][:, :], BASE_OF_Q[s][r], base[s][r][:, :]).then_inc(base_ready[s][r + 1], 1)

            def tanh_rest(s, i):
                dve.wait_ge(t32_ready[s], i)
                dve.tensor_tensor(t2[:, :], t32[:, :], t1[:, :], ALU.subtract).then_inc(t2_ready[s], 1)

            def advance(s, i, dst, ready):
                dve.wait_ge(rest_ready[s], i)
                dve.wait_ge(c_ready[s], i)
                stt(dst[:, :], ps_c[:, 0:W], STEP[s] / WSCALE, rest[:, :]).then_inc(ready, 1)

            def body(i, last_gru=False, last=False):
                first = isinstance(i, int) and i == 1
                dve.wait_ge(qraw_ready, i)
                if first:
                    dve.tensor_copy(q[0][:, :], qraw[:, :]).then_inc(q_ready[0], 1)
                else:
                    clip(q[0][:, :], qraw[:, :]).then_inc(q_ready[0], 1)
                dve.tensor_tensor(sq[:, :], qraw[:, :], qraw[:, :], ALU.mult).then_inc(sq_ready[0], 1)
                dve.wait_ge(q_ready[0], i)
                dve.wait_ge(base0p_ready, i)
                stt(base[0][0][:, :], q[0][:, :], SELF[0], base0p[:, :]).then_inc(base_ready[0][0], 1)
                dve.wait_ge(sq_ready[0], i)
                if first:
                    dve.tensor_tensor(cub[:, :], sq[:, :], q[0][:, :], ALU.mult).then_inc(cub_ready[0], 1)
                else:
                    stt(cub[:, :], sq[:, :], CLAMP * CLAMP, q[0][:, :], ALU.min, ALU.mult).then_inc(cub_ready[0], 1)
                tanh_rest(0, i)
                dve.wait_ge(cub_ready[0], i)
                dve.wait_ge(base_ready[0][0], i)
                stt(rest[:, :], cub[:, :], -STEP[0] / 3, base[0][0][:, :]).then_inc(rest_ready[0], 1)
                base_term(1, 0, i)
                advance(0, i, q[1], q_ready[1])

                for s in range(1, 4):
                    if s == 2:
                        base_term(3, 0, i)
                    if s == 3:
                        base_term(3, 2, i)
                    dve.wait_ge(q_ready[s], i)
                    stt(sq[:, :], q[s][:, :], STEP[s] / 3, q[s][:, :], ALU.mult, ALU.mult).then_inc(sq_ready[s], 1)
                    if s == 1 and not last:
                        dve.wait_ge(tr_ready, i)
                        stt(rh[:, :], tr[:, :], 1.0, ps_h[:, 0:W], ALU.add, ALU.mult).then_inc(m_ready, 1)
                    if s == 2:
                        base_term(2, 1, i)
                    if s == 3 and not last:
                        dve.wait_ge(pacc_ready[2], i)
                        stt(praw[:, :], q[3][:, :], P_OF_Q[3], pacc[2][:, :]).then_inc(praw_ready, 1)
                    dve.wait_ge(sq_ready[s], i)
                    stt(cub[:, :], sq[:, :], SELF[s], q[s][:, :], ALU.subtract, ALU.mult).then_inc(cub_ready[s], 1)
                    tanh_rest(s, i)
                    dve.wait_ge(cub_ready[s], i)
                    dve.wait_ge(base_ready[s][s], i)
                    dve.tensor_tensor(rest[:, :], base[s][s][:, :], cub[:, :], ALU.subtract).then_inc(rest_ready[s], 1)
                    if s == 1:
                        if not last:
                            dve.wait_ge(m_ready, i)
                            stt(npre[:, :], rh[:, :], 0.5, ps_i[:, 0:W]).then_inc(npre_ready, 1)
                        base_term(2, 0, i)
                    if s == 2:
                        base_term(3, 1, i)
                    if s == 3 and not last:
                        dve.wait_ge(praw_ready, i)
                        clip(p0[:, :], praw[:, :]).then_inc(p0_ready, 1)
                    if s < 3:
                        advance(s, i, q[s + 1], q_ready[s + 1])
                    else:
                        advance(s, i, qraw, qraw_ready)
                if not last:
                    dve.wait_ge(p0_ready, i + 1)
                    dve.wait_ge(sdrive0_ready, i)
                    base_of_p0().then_inc(base0p_ready, 1)

            loop(dve, body)
            dve.wait_ge(qraw_ready, T + 1)
            dve.wait_ge(out_ready, T - 1)
            clip(q[0][:, :], qraw[:, :]).then_inc(q_ready[0], 1)


def kernel(x, cond_2048, L0_cond_W_ih, L0_cond_W_hh, L0_cond_b_ih, L0_cond_b_hh, L1_cond_coupling, L1_cond_bias):
    import concourse.bacc as bacc
    import numpy as np
    from concourse.bass_utils import run_bass_kernel_spmd

    def features_first(a):
        a = np.asarray(a)
        return np.ascontiguousarray(np.moveaxis(a.reshape(HALVES, P, *a.shape[1:]), 0, 1))

    x, cond = np.asarray(x), np.asarray(cond_2048)
    nb, T, D = x.shape
    xt = features_first(x.transpose(2, 1, 0))
    arrays = {
        "x": np.ascontiguousarray(xt.transpose(0, 2, 1, 3)).reshape(P, T, W),
        "cond": features_first(cond.T).reshape(P, W),
        "wih": features_first(L0_cond_W_ih),
        "whh": features_first(L0_cond_W_hh),
        "bih": np.asarray(L0_cond_b_ih).reshape(1, -1),
        "bhh": np.asarray(L0_cond_b_hh).reshape(1, -1),
        "coup": features_first(np.asarray(L1_cond_coupling).T),
        "fbias": features_first(L1_cond_bias).reshape(P, HALVES),
    }
    nc = bacc.Bacc("TRN2", target_bir_lowering=False, num_devices=1)
    args = [nc.dram_tensor(k + "_dram", a.shape, mybir.dt.from_np(a.dtype), kind="ExternalInput").ap() for k, a in arrays.items()]
    out = nc.dram_tensor("out_dram", (T, P, W), mybir.dt.from_np(np.dtype("float32")), kind="ExternalOutput").ap()
    build(nc, *args, out)
    got = run_bass_kernel_spmd(nc, [{k + "_dram": a for k, a in arrays.items()}], core_ids=[0]).results[0]["out_dram"]
    return np.ascontiguousarray(np.asarray(got).reshape(T, P, HALVES, nb).transpose(3, 0, 2, 1)).reshape(nb, T, D)
```

```python
from contextlib import ExitStack

import concourse.bass as bass
from concourse import mybir


P = 128
B = 32
HALVES = 2
W = HALVES * B
WSCALE = 256.0
UNROLL = 7
XFIRST = 3

DT = 0.01
HALF = 0.5 * DT
EPS = 0.08
ALPHA = 0.7
BETA = 0.8
CLAMP = 20.0
X = HALF * EPS * BETA

GAM = DT * EPS / 6.0
E_SHARE = 1 + 2 * (1 - X) + 2 * (1 - X + X * X) + (1 - 2 * X + 2 * X**2 - 2 * X**3)
P_OF_P0 = 1.0 - GAM * E_SHARE * BETA
P_CONST = GAM * E_SHARE * ALPHA
P_OF_Q = [GAM * (1 - 2 * X + 2 * X**2 - 2 * X**3), GAM * (2 - 2 * X + 2 * X**2), GAM * (2 - 2 * X), GAM]

STEP = [HALF, HALF, DT, DT / 6.0]
UNIT = [WSCALE / s for s in STEP]
SHIFT = [0.0, 1.0, 1.0, 2.0 / 3.0]
BASE_OF_E = [0.0, -HALF * HALF * EPS, -DT * HALF * EPS * (1 - X), -DT * DT * EPS / 6 * (1 - X + X * X)]
BASE_OF_P0 = [UNIT[s] * (-STEP[s] - BETA * BASE_OF_E[s]) for s in range(4)]
BASE_CONST = [UNIT[s] * ALPHA * BASE_OF_E[s] for s in range(4)]
BASE_OF_Q = [
    [],
    [UNIT[1] * (1 - HALF * HALF * EPS)],
    [UNIT[2] * (1 + DT * HALF * EPS * X), UNIT[2] * -DT * HALF * EPS],
    [UNIT[3] * (-1 / 3 - DT * DT * EPS / 6 * X * X), UNIT[3] * (1 / 3 + DT * DT * EPS / 6 * X),
     UNIT[3] * (2 / 3 - DT * DT * EPS / 6)],
]
SELF = [1 + HALF, SHIFT[1] + HALF, SHIFT[2] + DT, SHIFT[3] + 1 / 3 + DT / 6]


def build(nc, x_in, cond_in, wih_in, whh_in, biases_in, coup_in, fbias_in, out):
    f32 = mybir.dt.float32
    f16 = mybir.dt.float16
    ALU = mybir.AluOpType
    ACT = mybir.ActivationFunctionType
    T = x_in.shape[1]
    N3 = wih_in.shape[2]
    ND = coup_in.shape[2]

    ctx = ExitStack()
    with ctx:

        def sb(name, shape, dt=f32):
            return ctx.enter_context(nc.sbuf_tensor(name, shape, dt))

        def pb(name):
            return ctx.enter_context(nc.psum_tensor(name, [P, 512], f32))

        def sem(name):
            return ctx.enter_context(nc.semaphore(name))

        x = sb("x", [P, T * W])
        xhl = sb("xhl", [P, T * 2 * W], f16)
        outb = sb("outb", [P, T * W])
        wih = sb("wih", [P, 2, N3])
        whh = sb("whh", [P, 2, N3])
        coup = sb("coup", [P, 2, ND])
        fbias = sb("fbias", [P, HALVES])
        brow = sb("brow", [P, N3])
        wih1, wih2 = sb("wih1", [P, 2, N3], f16), sb("wih2", [P, 2, N3], f16)
        whh1, whh2 = sb("whh1", [P, 2, N3], f16), sb("whh2", [P, 2, N3], f16)
        cp1, cp2 = sb("cp1", [P, 2, ND], f16), sb("cp2", [P, 2, ND], f16)
        bsp = sb("bsp", [P, N3], f16)
        pick_both, pick_ih, pick_hh = sb("pick_both", [P, B], f16), sb("pick_ih", [P, B], f16), sb("pick_hh", [P, B], f16)

        h, h1, h2 = sb("h", [P, W]), sb("h1", [P, W], f16), sb("h2", [P, W], f16)
        tr, tz, z, n = sb("tr", [P, W]), sb("tz", [P, W]), sb("z", [P, W]), sb("n", [P, W])
        rh, npre, dhn, zd = sb("rh", [P, W]), sb("npre", [P, W]), sb("dhn", [P, W]), sb("zd", [P, W])

        qraw = sb("qraw", [P, W])
        q = [sb(f"q{s}", [P, W]) for s in range(4)]
        p0, praw = sb("p0", [P, W]), sb("praw", [P, W])
        t1, t2 = sb("t1", [P, W], f16), sb("t2", [P, W], f16)
        sq, cub = sb("sq", [P, W]), sb("cub", [P, W])
        xb, drive = sb("xb", [P, W]), sb("drive", [P, W])
        sdrive, sdrive1 = sb("sdrive", [P, W]), sb("sdrive1", [P, W])
        sp0 = {s: sb(f"sp0_{s}", [P, W]) for s in (2, 3)}
        sq0 = {s: sb(f"sq0_{s}", [P, W]) for s in (2, 3)}
        base = [[sb(f"base{s}_{r}", [P, W]) for r in range(s + 1)] for s in range(4)]
        pq0 = sb("pq0", [P, W])
        pacc0 = sb("pacc0", [P, W])
        pacc = [sb(f"pacc_{r}", [P, W]) for r in range(3)]

        ps_first, ps_other = pb("ps_c_first"), pb("ps_c_other")
        ps_c = [ps_first, ps_other, ps_other, ps_other]
        ps_r, ps_z, ps_h, ps_i = pb("ps_r"), pb("ps_z"), pb("ps_h"), pb("ps_i")
        t32, q_act = pb("t32")[:, 0:W], pb("q_act")[:, 0:W]

        ld_x0, ld_x, ld_coup, ld_b, ld_state, ld_fb = (sem(k) for k in (
            "ld_x0", "ld_x", "ld_coup", "ld_b", "ld_state", "ld_fb"))
        ld_wih, ld_whh = [sem(f"ld_wih{k}") for k in range(2)], [sem(f"ld_whh{k}") for k in range(2)]
        brow_zero, picks, picks0, tables = sem("brow_zero"), sem("picks"), sem("picks0"), sem("tables")
        hi_x0, hi_wih, hi_whh, hi_coup, hi_b, hi_h = (sem(k) for k in ("hi_x0", "hi_wih", "hi_whh", "hi_coup", "hi_b", "hi_h"))
        lo_x0, lo_wih, lo_whh, lo_coup, lo_b, lo_h = (sem(k) for k in ("lo_x0", "lo_wih", "lo_whh", "lo_coup", "lo_b", "lo_h"))
        g_rz, g_h, g_r, g_rh, g_np, g_n, g_d, g_z, g_zd, g_hn, g_h1, g_xb, g_dr = (
            sem("g0_" + k) for k in ("rz", "h", "r", "rh", "np", "n", "d", "z", "zd", "hn", "h1", "xb", "dr"))
        rh_ready, h2_ready, qraw_ready, p0_ready, seed0_ready = (
            sem(k) for k in ("rh_ready", "h2_ready", "qraw_ready", "p0_ready", "seed0_ready"))
        sdrive_ready = sem("sdrive_ready")
        qact_ready = [sem(f"qact_ready{s}") for s in range(4)]
        seed_ready = [seed0_ready] + [sem(f"seed_ready{s}") for s in range(1, 4)]
        ps_c_open = sem("ps_c_open")
        tr_ready, zpre_ready, tz_ready, z_ready, m_ready, npre_ready, n_ready, dhn_ready, zd_ready, h_ready = (
            sem(k) for k in ("tr_ready", "zpre_ready", "tz_ready", "z_ready", "m_ready", "npre_ready", "n_ready", "dhn_ready",
                             "zd_ready", "h_ready"))
        h1_ready, sdrive0_ready = sem("h1_ready"), sem("sdrive0_ready")
        xlo_ready, xb_ready, drive_ready, xh_ready = (sem(k) for k in ("xlo_ready", "xb_ready", "drive_ready", "xh_ready"))
        sdrive1_ready = sem("sdrive1_ready")
        q_ready = [sem(f"q_ready{s}") for s in range(4)]
        t1_ready = [sem(f"t1_ready{s}") for s in range(4)]
        t32_ready = [sem(f"t32_ready{s}") for s in range(4)]
        t2_ready = [sem(f"t2_ready{s}") for s in range(4)]
        c_ready = [sem(f"c_ready{s}") for s in range(4)]
        sq_ready = [sem(f"sq_ready{s}") for s in range(4)]
        cub_ready = [sem(f"cub_ready{s}") for s in range(4)]
        sp0_ready = {s: sem(f"sp0_ready{s}") for s in (2, 3)}
        sq0_ready = {s: sem(f"sq0_ready{s}") for s in (2, 3)}
        base_ready = [[sem(f"base_ready{s}_{r}") for r in range(s + 1)] for s in range(4)]
        pq0_ready = sem("pq0_ready")
        pacc_ready = [sem(f"pacc_ready{r}") for r in range(3)]
        praw_ready = sem("praw_ready")
        out_ready, stored = sem("out_ready"), sem("stored")

        def at(t, width):
            return bass.ds(t * width, width)

        def xs(t):
            return x[:, at(t, W)]

        def xhi(t):
            return xhl[:, bass.ds(t * 2 * W, W)]

        def xlo(t):
            return xhl[:, bass.ds(t * 2 * W + W, W)]

        def loop(eng, body):
            start = T - 2 - (T - 3) // UNROLL * UNROLL
            for i in range(1, start):
                body(i)
            with eng.Fori(0, (T - 2 - start) // UNROLL) as r:
                i = eng.snap(r * UNROLL + start)
                for j in range(UNROLL):
                    body(i + j)
            body(T - 2, before_last_gru=True)
            body(T - 1, last_gru=True)
            body(T, last=True)

        block = ctx.enter_context(nc.Block())

        @block.sync
        def _(sp):
            sp.dma_start(h[:, :], cond_in).then_inc(ld_state, 16)
            for k in range(2):
                sp.dma_start(wih[:, k, :], wih_in[:, k, :]).then_inc(ld_wih[k], 16)
            for k in range(2):
                sp.dma_start(whh[:, k, :], whh_in[:, k, :]).then_inc(ld_whh[k], 16)
            sp.dma_start(coup[:, :, :], coup_in).then_inc(ld_coup, 16)
            sp.dma_start(x[:, XFIRST * W :], x_in[:, XFIRST:, :].rearrange("p t w -> p (t w)")).then_inc(ld_x, 16)

            def body(k):
                sp.wait_ge(out_ready, k)
                sp.dma_start(out[bass.ds(k - 1, 1), :, :].rearrange("o p w -> p (o w)"), outb[:, at(k - 1, W)]).then_inc(stored, 16)

            with sp.Fori(1, T + 1) as k:
                body(k)
            sp.wait_ge(stored, 16 * T)

        @block.gpsimd
        def _(pool):
            pool.memset(brow[:, :], 0.0).then_inc(brow_zero, 1)
            pool.memset(pick_both[:, :], 1.0).then_inc(picks, 1)
            pool.memset(pick_ih[:, :], 0.0).then_inc(picks0, 1)
            pool.memset(pick_hh[:, :], 0.0).then_inc(picks0, 1)
            pool.wait_ge(picks0, 2)
            for r in (0, 64):
                pool.memset(pick_ih[r : r + 32, :], 1.0).then_inc(picks, 1)
                pool.memset(pick_hh[r + 32 : r + 64, :], 1.0).then_inc(picks, 1)
            pool.wait_ge(g_h1, 1)
            pool.tensor_tensor(h2[:, :], h[:, :], h1[:, :], ALU.subtract).then_inc(h2_ready, 1)

            def add_q0(i):
                step = outb[:, at(i - 2, W)]
                pool.tensor_tensor(step, step, q[0][:, :], ALU.add).then_inc(out_ready, 1)

            def body(i, before_last_gru=False, last_gru=False, last=False):
                first = isinstance(i, int) and i == 1
                if not (first or last_gru or last):
                    pool.tensor_tensor(xlo(i + 1), xs(i + 1), xhi(i + 1), ALU.subtract).then_inc(xlo_ready, 1)
                pool.tensor_tensor(outb[:, at(i - 1, W)], xs(i - 1), h[:, :], ALU.add).then_inc(xh_ready, 1)
                for s in (2, 3):
                    pool.wait_ge(sp0_ready[s], i)
                    pool.tensor_tensor(base[s][0][:, :], sp0[s][:, :], sdrive[:, :], ALU.add).then_inc(base_ready[s][0], 1)
                    pool.wait_ge(sq0_ready[s], i)
                    pool.wait_ge(base_ready[s][0], i)
                    pool.tensor_tensor(base[s][1][:, :], sq0[s][:, :], base[s][0][:, :], ALU.add).then_inc(base_ready[s][1], 1)
                if last:
                    add_q0(i)
                    return
                pool.wait_ge(pq0_ready, i)
                pool.tensor_tensor(pacc[0][:, :], pacc0[:, :], pq0[:, :], ALU.add).then_inc(pacc_ready[0], 1)
                pool.wait_ge(n_ready, i)
                pool.tensor_tensor(dhn[:, :], h[:, :], n[:, :], ALU.subtract).then_inc(dhn_ready, 1)
                pool.wait_ge(dhn_ready, i)
                pool.wait_ge(z_ready, i)
                pool.tensor_tensor(zd[:, :], z[:, :], dhn[:, :], ALU.mult).then_inc(zd_ready, 1)
                pool.wait_ge(zd_ready, i)
                pool.tensor_tensor(h[:, :], n[:, :], zd[:, :], ALU.add).then_inc(h_ready, 1)
                pool.wait_ge(h_ready, i)
                pool.wait_ge(xb_ready, i)
                pool.tensor_tensor(drive[:, :], xb[:, :], h[:, :], ALU.add).then_inc(drive_ready, 1)
                if not first:
                    add_q0(i)
                if not last_gru:
                    pool.wait_ge(h1_ready, i)
                    pool.tensor_tensor(h2[:, :], h[:, :], h1[:, :], ALU.subtract).then_inc(h2_ready, 1)

            loop(pool, body)
            pool.wait_ge(q_ready[0], T + 1)
            pool.wait_ge(xh_ready, T)
            pool.tensor_tensor(outb[:, at(T - 1, W)], outb[:, at(T - 1, W)], q[0][:, :], ALU.add).then_inc(out_ready, 1)

        @block.tensor
        def _(pe):
            r_cols, z_cols, n_cols = 0, HALVES, 2 * HALVES

            def mm(ps, half, w, k, tile, mov, start):
                return pe.matmul(ps[:, half * B : (half + 1) * B], w[:, k, tile * P : (tile + 1) * P], mov,
                                 start=start, stop=True, skip_group_check=True)

            def x_part(ps, first_tile, t, pick):
                for half in range(HALVES):
                    tile = first_tile + half
                    pe.matmul(ps[:, half * B : (half + 1) * B], bsp[:, tile * P : (tile + 1) * P], pick[:, :],
                              start=half == 0, stop=True, skip_group_check=True)
                    for k in range(2):
                        xk = [xhl[:, bass.ds(t * 2 * W + part * W + k * B, B)] for part in range(2)]
                        mm(ps, half, wih1, k, tile, xk[0], False)
                        mm(ps, half, wih2, k, tile, xk[0], False)
                        last = mm(ps, half, wih1, k, tile, xk[1], False)
                return last

            def hn_bias():
                for half in range(HALVES):
                    tile = n_cols + half
                    last = pe.matmul(ps_h[:, half * B : (half + 1) * B], bsp[:, tile * P : (tile + 1) * P], pick_hh[:, :],
                                     start=half == 0, stop=True, skip_group_check=True)
                return last

            def h_part(ps, first_tile, parts=(1, 2)):
                for part in parts:
                    for half in range(HALVES):
                        tile = first_tile + half
                        for k in range(2):
                            if part == 1:
                                mm(ps, half, whh1, k, tile, h1[:, k * B : (k + 1) * B], False)
                                last = mm(ps, half, whh2, k, tile, h1[:, k * B : (k + 1) * B], False)
                            else:
                                last = mm(ps, half, whh1, k, tile, h2[:, k * B : (k + 1) * B], False)
                return last

            pe.wait_ge(picks, 5)
            pe.wait_ge(lo_b, 1)
            for ps in (ps_first, ps_other):
                for half in range(HALVES):
                    pe.matmul(ps[:, half * B : (half + 1) * B], bsp[:, 0:P], pick_both[:, :], start=half == 0, stop=True,
                              skip_group_check=True).then_inc(ps_c_open, 1)
            pe.wait_ge(lo_x0, 1)
            pe.wait_ge(lo_wih, 2)
            x_part(ps_r, r_cols, 0, pick_both)
            x_part(ps_i, n_cols, 0, pick_ih)
            x_part(ps_z, z_cols, 0, pick_both)
            hn_bias()
            pe.wait_ge(lo_whh, 2)
            pe.wait_ge(lo_h, 1)
            h_part(ps_r, r_cols)
            h_part(ps_z, z_cols).then_inc(g_rz, 1)
            h_part(ps_h, n_cols).then_inc(g_h, 1)
            pe.wait_ge(g_z, 1)
            x_part(ps_r, r_cols, 1, pick_both)
            x_part(ps_z, z_cols, 1, pick_both)
            pe.wait_ge(g_np, 1)
            x_part(ps_i, n_cols, 1, pick_ih)
            hn_bias()
            pe.wait_ge(h2_ready, 1)
            h_part(ps_r, r_cols)
            h_part(ps_h, n_cols).then_inc(rh_ready, 1)

            def coupling_hi(ps):
                for half in range(HALVES):
                    for k in range(2):
                        tk = t1[:, k * B : (k + 1) * B]
                        mm(ps, half, cp1, k, half, tk, False)
                        mm(ps, half, cp2, k, half, tk, False)

            def coupling_lo(ps):
                for half in range(HALVES):
                    for k in range(2):
                        last = mm(ps, half, cp1, k, half, t2[:, k * B : (k + 1) * B], False)
                return last

            pe.wait_ge(lo_coup, 1)

            def body(i, before_last_gru=False, last_gru=False, last=False):
                first = isinstance(i, int) and i == 1
                for s in range(4):
                    pe.wait_ge(seed_ready[s], i)
                    pe.wait_ge(t1_ready[s], i)
                    coupling_hi(ps_c[s])
                    pe.wait_ge(t2_ready[s], i)
                    coupling_lo(ps_c[s]).then_inc(c_ready[s], 1)
                    if last:
                        continue
                    if s == 0:
                        h_part(ps_z, z_cols).then_inc(zpre_ready, 1)
                        if not last_gru:
                            pe.wait_ge(tr_ready, i)
                            if not first:
                                pe.wait_ge(xlo_ready, i - 1)
                            x_part(ps_r, r_cols, i + 1, pick_both)
                    if last_gru:
                        continue
                    if s == 1:
                        pe.wait_ge(tz_ready, i)
                        x_part(ps_z, z_cols, i + 1, pick_both)
                    if s == 2:
                        pe.wait_ge(npre_ready, i)
                        x_part(ps_i, n_cols, i + 1, pick_ih)
                        hn_bias()
                    if s == 3:
                        pe.wait_ge(h1_ready, i)
                        h_part(ps_r, r_cols, (1,))
                        h_part(ps_h, n_cols, (1,))
                        pe.wait_ge(h2_ready, i + 1)
                        h_part(ps_r, r_cols, (2,))
                        h_part(ps_h, n_cols, (2,)).then_inc(rh_ready, 1)

            loop(pe, body)

        @block.scalar
        def _(act):
            act.dma_start(x[:, 0 : XFIRST * W], x_in[:, 0:XFIRST, :].rearrange("p t w -> p (t w)")).then_inc(ld_x0, 16)
            act.wait_ge(brow_zero, 1)
            act.dma_start(brow[0:P:32, :], biases_in).then_inc(ld_b, 16)
            act.dma_start(fbias[:, :], fbias_in).then_inc(ld_fb, 16)

            def affine(out_, in_, scale, shift=0.0):
                return act.activation(out_, in_, ACT.Copy, scale=scale, bias=shift)

            def x_and_bias(t):
                for k in range(HALVES):
                    last = act.activation(xb[:, k * B : (k + 1) * B], x[:, bass.ds(t * W + k * B, B)], ACT.Identity,
                                          bias=fbias[:, k : k + 1])
                return last

            act.wait_ge(picks, 1)
            act.activation(tr[:, 0:B], pick_both[:, :], ACT.Tanh).then_inc(tables, 1)

            act.wait_ge(ld_state, 16)
            affine(h1[:, :], h[:, :], 1.0).then_inc(hi_h, 1)
            act.wait_ge(ld_x0, 16)
            xv = x[:, 0 : XFIRST * W].rearrange("p (t w) -> p t w", w=W)
            xhlv = xhl[:, 0 : XFIRST * 2 * W].rearrange("p (t a w) -> p t a w", a=2, w=W)
            affine(xhlv[:, :, 0, :], xv, 1.0).then_inc(hi_x0, 1)
            act.wait_ge(ld_b, 16)
            affine(bsp[:, :], brow[:, :], WSCALE).then_inc(hi_b, 1)
            for k in range(2):
                act.wait_ge(ld_wih[k], 16)
                affine(wih1[:, k, :], wih[:, k, :], WSCALE).then_inc(hi_wih, 1)
            for k in range(2):
                act.wait_ge(ld_whh[k], 16)
                affine(whh1[:, k, :], whh[:, k, :], WSCALE).then_inc(hi_whh, 1)
            act.wait_ge(ld_coup, 16)
            affine(cp1[:, :, :], coup[:, :, :], WSCALE).then_inc(hi_coup, 1)
            act.wait_ge(ld_fb, 16)
            x_and_bias(0).then_inc(g_xb, 1)

            act.wait_ge(g_rz, 1)
            act.activation(tr[:, :], ps_r[:, 0:W], ACT.Tanh, scale=0.5 / WSCALE).then_inc(g_r, 1)
            act.activation(tz[:, :], ps_z[:, 0:W], ACT.Tanh, scale=0.5 / WSCALE).then_inc(g_r, 1)
            act.wait_ge(g_r, 2)
            affine(z[:, :], tz[:, :], 0.5, 0.5).then_inc(g_z, 1)
            act.wait_ge(g_np, 1)
            act.activation(n[:, :], npre[:, :], ACT.Tanh, scale=1.0 / WSCALE).then_inc(g_n, 1)
            act.wait_ge(g_hn, 1)
            affine(h1[:, :], h[:, :], 1.0).then_inc(g_h1, 1)
            act.wait_ge(g_dr, 1)
            affine(sdrive[:, :], drive[:, :], WSCALE).then_inc(sdrive_ready, 1)
            affine(sdrive1[:, :], drive[:, :], WSCALE, BASE_CONST[1]).then_inc(sdrive_ready, 1)

            def body(i, before_last_gru=False, last_gru=False, last=False):
                first = isinstance(i, int) and i == 1
                for s in range(4):
                    act.wait_ge(qact_ready[s], i)
                    act.activation(t1[:, :], q_act, ACT.Tanh).then_inc(t1_ready[s], 1)
                    act.activation(t32, q_act, ACT.Tanh).then_inc(t32_ready[s], 1)
                    if s == 0:
                        act.wait_ge(q_ready[0], i)
                    act.activation(sq[:, :], q_act if s else q[0][:, :], ACT.Square,
                                   scale=(STEP[s] / 3) ** 0.5).then_inc(sq_ready[s], 1)
                    if s == 0:
                        if not last:
                            act.wait_ge(rh_ready, i)
                            act.activation(tr[:, :], ps_r[:, 0:W], ACT.Tanh, scale=0.5 / WSCALE).then_inc(tr_ready, 1)
                        act.wait_ge(p0_ready, i)
                        for r in (2, 3):
                            affine(sp0[r][:, :], p0[:, :], BASE_OF_P0[r], BASE_CONST[r]).then_inc(sp0_ready[r], 1)
                            affine(sq0[r][:, :], q[0][:, :], BASE_OF_Q[r][0]).then_inc(sq0_ready[r], 1)
                    if last:
                        continue
                    if s == 1:
                        affine(pacc0[:, :], p0[:, :], P_OF_P0, P_CONST)
                        affine(pq0[:, :], q[0][:, :], P_OF_Q[0]).then_inc(pq0_ready, 1)
                        act.wait_ge(zpre_ready, i)
                        act.activation(tz[:, :], ps_z[:, 0:W], ACT.Tanh, scale=0.5 / WSCALE).then_inc(tz_ready, 1)
                        act.wait_ge(tz_ready, i)
                        affine(z[:, :], tz[:, :], 0.5, 0.5).then_inc(z_ready, 1)
                        act.wait_ge(npre_ready, i)
                        act.activation(n[:, :], npre[:, :], ACT.Tanh, scale=1.0 / WSCALE).then_inc(n_ready, 1)
                    if s == 2:
                        if first:
                            act.wait_ge(ld_x, 16)
                        if not (before_last_gru or last_gru):
                            affine(xhi(i + 2), xs(i + 2), 1.0)
                        x_and_bias(i).then_inc(xb_ready, 1)
                    if s == 3:
                        if not last_gru:
                            act.wait_ge(h_ready, i)
                            affine(h1[:, :], h[:, :], 1.0).then_inc(h1_ready, 1)
                        act.wait_ge(drive_ready, i)
                        affine(sdrive[:, :], drive[:, :], WSCALE).then_inc(sdrive0_ready, 1)
                        affine(sdrive1[:, :], drive[:, :], WSCALE, BASE_CONST[1]).then_inc(sdrive1_ready, 1)

            loop(act, body)

        @block.vector
        def _(dve):
            def stt(out_, in0, scalar, in1, op0=ALU.mult, op1=ALU.add):
                return dve.scalar_tensor_tensor(out_, in0, scalar, in1, op0, op1)

            def clip(out_, in_):
                return dve.tensor_scalar(out_, in_, CLAMP, -CLAMP, ALU.min, ALU.max)

            def seed_0():
                return stt(ps_c[0][:, 0:W], p0[:, :], BASE_OF_P0[0], sdrive[:, :])

            dve.wait_ge(ld_state, 16)
            dve.tensor_copy(q_act, h[:, :]).then_inc(qact_ready[0], 1)
            dve.tensor_copy(qraw[:, :], h[:, :]).then_inc(qraw_ready, 1)
            dve.tensor_copy(p0[:, :], h[:, :]).then_inc(p0_ready, 1)

            dve.wait_ge(hi_h, 1)
            dve.tensor_tensor(h2[:, :], h[:, :], h1[:, :], ALU.subtract).then_inc(lo_h, 1)
            dve.wait_ge(hi_x0, 1)
            xv = x[:, 0 : XFIRST * W].rearrange("p (t w) -> p t w", w=W)
            xhlv = xhl[:, 0 : XFIRST * 2 * W].rearrange("p (t a w) -> p t a w", a=2, w=W)
            dve.tensor_tensor(xhlv[:, :, 1, :], xv, xhlv[:, :, 0, :], ALU.subtract).then_inc(lo_x0, 1)
            dve.wait_ge(hi_b, 1)
            stt(bsp[64:128, :], brow[64:128, :], WSCALE, bsp[64:128, :], op1=ALU.subtract).then_inc(lo_b, 1)
            for k in range(2):
                dve.wait_ge(hi_wih, k + 1)
                stt(wih2[:, k, :], wih[:, k, :], WSCALE, wih1[:, k, :], op1=ALU.subtract).then_inc(lo_wih, 1)
            for k in range(2):
                dve.wait_ge(hi_whh, k + 1)
                stt(whh2[:, k, :], whh[:, k, :], WSCALE, whh1[:, k, :], op1=ALU.subtract).then_inc(lo_whh, 1)
            dve.wait_ge(hi_coup, 1)
            stt(cp2[:, :, :], coup[:, :, :], WSCALE, cp1[:, :, :], op1=ALU.subtract).then_inc(lo_coup, 1)

            dve.wait_ge(g_h, 1)
            dve.wait_ge(g_r, 2)
            stt(rh[:, :], tr[:, :], 1.0, ps_h[:, 0:W], ALU.add, ALU.mult).then_inc(g_rh, 1)
            dve.wait_ge(g_rh, 1)
            stt(npre[:, :], rh[:, :], 0.5, ps_i[:, 0:W]).then_inc(g_np, 1)
            dve.wait_ge(g_n, 1)
            dve.tensor_tensor(dhn[:, :], h[:, :], n[:, :], ALU.subtract).then_inc(g_d, 1)
            dve.wait_ge(g_d, 1)
            dve.wait_ge(g_z, 1)
            dve.tensor_tensor(zd[:, :], z[:, :], dhn[:, :], ALU.mult).then_inc(g_zd, 1)
            dve.wait_ge(g_zd, 1)
            dve.tensor_tensor(h[:, :], n[:, :], zd[:, :], ALU.add).then_inc(g_hn, 1)
            dve.wait_ge(g_hn, 1)
            dve.wait_ge(g_xb, 1)
            dve.tensor_tensor(drive[:, :], xb[:, :], h[:, :], ALU.add).then_inc(g_dr, 1)
            dve.wait_ge(sdrive_ready, 2)
            dve.wait_ge(ps_c_open, 4)
            seed_0().then_inc(seed0_ready, 1)

            def base_term(s, r, i):
                dve.wait_ge(base_ready[s][r], i)
                return stt(base[s][r + 1][:, :], q[r][:, :], BASE_OF_Q[s][r], base[s][r][:, :]).then_inc(base_ready[s][r + 1], 1)

            def tanh_rest(s, i):
                dve.wait_ge(t32_ready[s], i)
                dve.tensor_tensor(t2[:, :], t32[:, :], t1[:, :], ALU.subtract).then_inc(t2_ready[s], 1)

            def advance(s, i, dst, dst_ready, act_ready):
                for ready in (cub_ready, c_ready) if s == 0 else (c_ready, cub_ready):
                    dve.wait_ge(ready[s], i)
                stt(q_act, ps_c[s][:, 0:W], STEP[s] / WSCALE, cub[:, :], op1=ALU.subtract).then_inc(act_ready, 1)
                stt(dst[:, :], ps_c[s][:, 0:W], STEP[s] / WSCALE, cub[:, :], op1=ALU.subtract).then_inc(dst_ready, 1)

            def cube(s, i):
                dve.wait_ge(sq_ready[s], i)
                dve.wait_ge(q_ready[s], i)
                stt(cub[:, :], sq[:, :], SELF[s], q[s][:, :], ALU.subtract, ALU.mult).then_inc(cub_ready[s], 1)

            def seed(s, i):
                dve.wait_ge(q_ready[s], i)
                dve.wait_ge(base_ready[s][s], i)
                stt(ps_c[s][:, 0:W], q[s][:, :], -SHIFT[s] * UNIT[s], base[s][s][:, :]).then_inc(seed_ready[s], 1)

            def body(i, before_last_gru=False, last_gru=False, last=False):
                first = isinstance(i, int) and i == 1
                dve.wait_ge(qraw_ready, i)
                if first:
                    dve.tensor_copy(q[0][:, :], qraw[:, :]).then_inc(q_ready[0], 1)
                else:
                    if last:
                        dve.wait_ge(out_ready, T - 2)
                    else:
                        dve.wait_ge(h2_ready, i)
                    clip(q[0][:, :], qraw[:, :]).then_inc(q_ready[0], 1)
                tanh_rest(0, i)
                if not first:
                    dve.wait_ge(sdrive1_ready, i - 1)
                stt(base[1][0][:, :], p0[:, :], BASE_OF_P0[1], sdrive1[:, :]).then_inc(base_ready[1][0], 1)
                cube(0, i)
                base_term(1, 0, i)
                advance(0, i, q[1], q_ready[1], qact_ready[1])
                if not last:
                    dve.wait_ge(tr_ready, i)
                    stt(rh[:, :], tr[:, :], 1.0, ps_h[:, 0:W], ALU.add, ALU.mult).then_inc(m_ready, 1)
                seed(1, i)
                tanh_rest(1, i)
                cube(1, i)
                if not last:
                    dve.wait_ge(m_ready, i)
                    stt(npre[:, :], rh[:, :], 0.5, ps_i[:, 0:W]).then_inc(npre_ready, 1)
                base_term(2, 1, i)
                advance(1, i, q[2], q_ready[2], qact_ready[2])
                base_term(3, 1, i)
                seed(2, i)
                tanh_rest(2, i)
                cube(2, i)
                base_term(3, 2, i)
                if not last:
                    dve.wait_ge(pacc_ready[0], i)
                    stt(pacc[1][:, :], q[1][:, :], P_OF_Q[1], pacc[0][:, :]).then_inc(pacc_ready[1], 1)
                advance(2, i, q[3], q_ready[3], qact_ready[3])
                if not last:
                    dve.wait_ge(pacc_ready[1], i)
                    stt(pacc[2][:, :], q[2][:, :], P_OF_Q[2], pacc[1][:, :]).then_inc(pacc_ready[2], 1)
                seed(3, i)
                tanh_rest(3, i)
                if not last:
                    dve.wait_ge(pacc_ready[2], i)
                    stt(praw[:, :], q[3][:, :], P_OF_Q[3], pacc[2][:, :]).then_inc(praw_ready, 1)
                cube(3, i)
                if not last:
                    dve.wait_ge(praw_ready, i)
                    clip(p0[:, :], praw[:, :]).then_inc(p0_ready, 1)
                advance(3, i, qraw, qraw_ready, qact_ready[0])
                if not last:
                    dve.wait_ge(p0_ready, i + 1)
                    dve.wait_ge(sdrive0_ready, i)
                    seed_0().then_inc(seed0_ready, 1)

            loop(dve, body)
            dve.wait_ge(qraw_ready, T + 1)
            dve.wait_ge(out_ready, T - 1)
            clip(q[0][:, :], qraw[:, :]).then_inc(q_ready[0], 1)


def kernel(x, cond_2048, L0_cond_W_ih, L0_cond_W_hh, L0_cond_b_ih, L0_cond_b_hh, L1_cond_coupling, L1_cond_bias):
    import concourse.bacc as bacc
    import numpy as np
    from concourse.bass_utils import run_bass_kernel_spmd

    def features_first(a):
        a = np.asarray(a)
        return np.ascontiguousarray(np.moveaxis(a.reshape(HALVES, P, *a.shape[1:]), 0, 1))

    x, cond = np.asarray(x), np.asarray(cond_2048)
    nb, T, D = x.shape
    xt = features_first(x.transpose(2, 1, 0))
    arrays = {
        "x": np.ascontiguousarray(xt.transpose(0, 2, 1, 3)).reshape(P, T, W),
        "cond": features_first(cond.T).reshape(P, W),
        "wih": features_first(L0_cond_W_ih),
        "whh": features_first(L0_cond_W_hh),
        "biases": np.stack([L0_cond_b_ih, L0_cond_b_hh] * 2),
        "coup": features_first(np.asarray(L1_cond_coupling).T),
        "fbias": features_first(L1_cond_bias).reshape(P, HALVES),
    }
    nc = bacc.Bacc("TRN2", target_bir_lowering=False, num_devices=1)
    args = [nc.dram_tensor(k + "_dram", a.shape, mybir.dt.from_np(a.dtype), kind="ExternalInput").ap() for k, a in arrays.items()]
    out = nc.dram_tensor("out_dram", (T, P, W), mybir.dt.from_np(np.dtype("float32")), kind="ExternalOutput").ap()
    build(nc, *args, out)
    got = run_bass_kernel_spmd(nc, [{k + "_dram": a for k, a in arrays.items()}], core_ids=[0]).results[0]["out_dram"]
    return np.ascontiguousarray(np.asarray(got).reshape(T, P, HALVES, nb).transpose(3, 0, 2, 1)).reshape(nb, T, D)
```

```python
from contextlib import ExitStack

import concourse.bass as bass
from concourse import mybir


P = 128
B = 32
HALVES = 2
W = HALVES * B
WSCALE = 256.0
UNROLL = 7
XFIRST = 3

DT = 0.01
HALF = 0.5 * DT
EPS = 0.08
ALPHA = 0.7
BETA = 0.8
CLAMP = 20.0
X = HALF * EPS * BETA

GAM = DT * EPS / 6.0
E_SHARE = 1 + 2 * (1 - X) + 2 * (1 - X + X * X) + (1 - 2 * X + 2 * X**2 - 2 * X**3)
P_OF_P0 = 1.0 - GAM * E_SHARE * BETA
P_CONST = GAM * E_SHARE * ALPHA
P_OF_Q = [GAM * (1 - 2 * X + 2 * X**2 - 2 * X**3), GAM * (2 - 2 * X + 2 * X**2), GAM * (2 - 2 * X), GAM]

STEP = [HALF, HALF, DT, DT / 6.0]
UNIT = [WSCALE / s for s in STEP]
SHIFT = [0.0, 1.0, 1.0, 2.0 / 3.0]
BASE_OF_E = [0.0, -HALF * HALF * EPS, -DT * HALF * EPS * (1 - X), -DT * DT * EPS / 6 * (1 - X + X * X)]
BASE_OF_P0 = [UNIT[s] * (-STEP[s] - BETA * BASE_OF_E[s]) for s in range(4)]
BASE_CONST = [UNIT[s] * ALPHA * BASE_OF_E[s] for s in range(4)]
BASE_OF_Q = [
    [],
    [UNIT[1] * (1 - HALF * HALF * EPS)],
    [UNIT[2] * (1 + DT * HALF * EPS * X), UNIT[2] * -DT * HALF * EPS],
    [UNIT[3] * (-1 / 3 - DT * DT * EPS / 6 * X * X), UNIT[3] * (1 / 3 + DT * DT * EPS / 6 * X),
     UNIT[3] * (2 / 3 - DT * DT * EPS / 6)],
]
SELF = [1 + HALF, SHIFT[1] + HALF, SHIFT[2] + DT, SHIFT[3] + 1 / 3 + DT / 6]


def build(nc, x_in, cond_in, wih_in, whh_in, biases_in, coup_in, fbias_in, out):
    f32 = mybir.dt.float32
    f16 = mybir.dt.float16
    ALU = mybir.AluOpType
    ACT = mybir.ActivationFunctionType
    T = x_in.shape[1]
    N3 = wih_in.shape[2]
    ND = coup_in.shape[2]

    ctx = ExitStack()
    with ctx:

        def sb(name, shape, dt=f32):
            return ctx.enter_context(nc.sbuf_tensor(name, shape, dt))

        def pb(name):
            return ctx.enter_context(nc.psum_tensor(name, [P, 512], f32))

        def sem(name):
            return ctx.enter_context(nc.semaphore(name))

        x = sb("x", [P, T * W])
        xhl = sb("xhl", [P, T * 2 * W], f16)
        outb = sb("outb", [P, T * W])
        wih = sb("wih", [P, 2, N3])
        whh = sb("whh", [P, 2, N3])
        coup = sb("coup", [P, 2, ND])
        fbias = sb("fbias", [P, HALVES])
        brow, brow_s, coup_s = sb("brow", [P, N3]), sb("brow_s", [P, N3]), sb("coup_s", [P, ND])
        wih1, wih2 = sb("wih1", [P, 2, N3], f16), sb("wih2", [P, 2, N3], f16)
        whh1, whh2 = sb("whh1", [P, 2, N3], f16), sb("whh2", [P, 2, N3], f16)
        cp1, cp2 = sb("cp1", [P, 2, ND], f16), sb("cp2", [P, 2, ND], f16)
        bsp = sb("bsp", [P, N3], f16)
        pick_both, pick_ih, pick_hh = sb("pick_both", [P, B], f16), sb("pick_ih", [P, B], f16), sb("pick_hh", [P, B], f16)

        h, h1, h2 = sb("h", [P, W]), sb("h1", [P, W], f16), sb("h2", [P, W], f16)
        tr, tz, z, n = sb("tr", [P, W]), sb("tz", [P, W]), sb("z", [P, W]), sb("n", [P, W])
        omz, zh, xbzh, nz, p0_part = (sb(k, [P, W]) for k in ("omz", "zh", "xbzh", "nz", "p0_part"))
        rh, npre, dhn, zd = sb("rh", [P, W]), sb("npre", [P, W]), sb("dhn", [P, W]), sb("zd", [P, W])

        qraw = sb("qraw", [P, W])
        q = [sb(f"q{s}", [P, W]) for s in range(4)]
        p0, praw = sb("p0", [P, W]), sb("praw", [P, W])
        t, t2 = sb("t", [P, W]), sb("t2", [P, W], f16)
        t1 = t[:, :].bitcast(mybir.dt.bfloat16)[:, 1 : 2 * W : 2]
        sq, cub = sb("sq", [P, W]), sb("cub", [P, W])
        xb, drive = sb("xb", [P, W]), sb("drive", [P, W])
        sdrive, sdrive1 = sb("sdrive", [P, W]), sb("sdrive1", [P, W])
        sp0 = {s: sb(f"sp0_{s}", [P, W]) for s in (2, 3)}
        sq0 = {s: sb(f"sq0_{s}", [P, W]) for s in (2, 3)}
        base = {s: [sb(f"base{s}_{r}", [P, W]) for r in range(s + 1)] for s in (1, 2, 3)}
        pacc0, pq0 = sb("pacc0", [P, W]), sb("pq0", [P, W])
        pacc = [sb(f"pacc_{r}", [P, W]) for r in range(3)]

        ps_first, ps_other = pb("ps_c_first"), pb("ps_c_other")
        ps_c = [ps_first, ps_other, ps_other, ps_other]
        ps_r, ps_z, ps_h, ps_i = pb("ps_r"), pb("ps_z"), pb("ps_h"), pb("ps_i")
        ps_unread = pb("ps_unread")

        ld_x0, ld_x, ld_coup, ld_b, ld_state, ld_fb = (sem(k) for k in (
            "ld_x0", "ld_x", "ld_coup", "ld_b", "ld_state", "ld_fb"))
        ld_wih, ld_whh = [sem(f"ld_wih{k}") for k in range(2)], [sem(f"ld_whh{k}") for k in range(2)]
        brow_zero, picks, picks0, tables = sem("brow_zero"), sem("picks"), sem("picks0"), sem("tables")
        hi_x0, hi_wih, hi_whh, hi_coup, hi_b, hi_h = (sem(k) for k in ("hi_x0", "hi_wih", "hi_whh", "hi_coup", "hi_b", "hi_h"))
        lo_x0, lo_wih, lo_whh, lo_coup, lo_b, lo_h = (sem(k) for k in ("lo_x0", "lo_wih", "lo_whh", "lo_coup", "lo_b", "lo_h"))
        g0_r, g0_tr, g0_hn, g0_z, g0_tz, g0_zs, g0_rh, g0_npre, g0_n, g0_zh = (
            sem("g0_" + k) for k in ("r", "tr", "hn", "z", "tz", "zs", "rh", "npre", "n", "zh"))
        g0_xbzh, g0_nz, g0_h, g0_h1, g0_h2, g0_xb, g0_drive, g0_sdrive, g0_sdrive1, g0_p0 = (
            sem("g0_" + k) for k in ("xbzh", "nz", "h", "h1", "h2", "xb", "drive", "sdrive", "sdrive1", "p0"))
        brow_scaled, coup_scaled, p0_part_ready = sem("brow_scaled"), sem("coup_scaled"), sem("p0_part_ready")
        ps_c_open = sem("ps_c_open")
        rh_ready, seed_ready = sem("rh_ready"), [sem(f"seed_ready{s}") for s in range(4)]
        tr_ready, zpre_ready, tz_ready, z_ready, m_ready, npre_ready, n_ready, dhn_ready, zd_ready, h_ready = (
            sem(k) for k in ("tr_ready", "zpre_ready", "tz_ready", "z_ready", "m_ready", "npre_ready", "n_ready", "dhn_ready",
                             "zd_ready", "h_ready"))
        h1_ready, h2_ready, qraw_ready, p0_ready = (sem(k) for k in ("h1_ready", "h2_ready", "qraw_ready", "p0_ready"))
        xlo_ready, xb_ready, drive_ready, xh_ready = (sem(k) for k in ("xlo_ready", "xb_ready", "drive_ready", "xh_ready"))
        sdrive_ready, sdrive1_ready = sem("sdrive_ready"), sem("sdrive1_ready")
        q_ready = [sem(f"q_ready{s}") for s in range(4)]
        t_ready = [sem(f"t_ready{s}") for s in range(4)]
        t2_ready = [sem(f"t2_ready{s}") for s in range(4)]
        c_ready = [sem(f"c_ready{s}") for s in range(4)]
        sq_ready = [sem(f"sq_ready{s}") for s in range(4)]
        cub_ready = [sem(f"cub_ready{s}") for s in range(4)]
        sp0_ready = {s: sem(f"sp0_ready{s}") for s in (2, 3)}
        sq0_ready = {s: sem(f"sq0_ready{s}") for s in (2, 3)}
        base_ready = {s: [sem(f"base_ready{s}_{r}") for r in range(s + 1)] for s in (1, 2, 3)}
        pq0_ready = sem("pq0_ready")
        pacc_ready = [sem(f"pacc_ready{r}") for r in range(3)]
        praw_ready = sem("praw_ready")
        out_ready, stored = sem("out_ready"), sem("stored")

        def at(t, width):
            return bass.ds(t * width, width)

        H = N3 // 3
        whh_pieces = [(0, slice(0, 2 * H)), (0, slice(2 * H, N3)), (1, slice(0, H)), (1, slice(2 * H, N3)), (1, slice(H, 2 * H))]

        def xs(t):
            return x[:, at(t, W)]

        def xhi(t):
            return xhl[:, bass.ds(t * 2 * W, W)]

        def xlo(t):
            return xhl[:, bass.ds(t * 2 * W + W, W)]

        def loop(eng, body):
            start = T - 2 - (T - 3) // UNROLL * UNROLL
            for i in range(1, start):
                body(i)
            with eng.Fori(start, T - 1 - UNROLL, UNROLL) as i:
                for j in range(UNROLL):
                    body(i + j)
            body(T - 2, before_last_gru=True)
            body(T - 1, last_gru=True)
            body(T, last=True)

        block = ctx.enter_context(nc.Block())

        @block.sync
        def _(sp):
            sp.dma_start(h[:, :], cond_in).then_inc(ld_state, 16)
            sp.dma_start(x[:, 0 : XFIRST * W], x_in[:, 0:XFIRST, :].rearrange("p t w -> p (t w)")).then_inc(ld_x0, 16)
            sp.wait_ge(brow_zero, 1)
            sp.dma_start(brow[0:P:32, :], biases_in).then_inc(ld_b, 16)
            sp.dma_start(wih[:, 0, :], wih_in[:, 0, :]).then_inc(ld_wih[0], 16)
            sp.dma_start(fbias[:, :], fbias_in).then_inc(ld_fb, 16)
            sp.dma_start(wih[:, 1, :], wih_in[:, 1, :]).then_inc(ld_wih[1], 16)
            for k in range(2):
                sp.dma_start(whh[:, k, :], whh_in[:, k, :]).then_inc(ld_whh[k], 16)
            sp.dma_start(coup[:, :, :], coup_in).then_inc(ld_coup, 16)
            sp.dma_start(x[:, XFIRST * W :], x_in[:, XFIRST:, :].rearrange("p t w -> p (t w)")).then_inc(ld_x, 16)

            def body(k):
                sp.wait_ge(out_ready, k)
                sp.dma_start(out[bass.ds(k - 1, 1), :, :].rearrange("o p w -> p (o w)"), outb[:, at(k - 1, W)]).then_inc(stored, 16)

            with sp.Fori(1, T + 1) as k:
                body(k)
            sp.wait_ge(stored, 16 * T)

        @block.gpsimd
        def _(pool):
            pool.memset(pick_both[:, :], 1.0).then_inc(picks, 1)
            pool.memset(brow[:, :], 0.0).then_inc(brow_zero, 1)
            pool.memset(pick_ih[:, :], 0.0).then_inc(picks0, 1)
            pool.memset(pick_hh[:, :], 0.0).then_inc(picks0, 1)
            pool.wait_ge(picks0, 2)
            for r in (0, 64):
                pool.memset(pick_ih[r : r + 32, :], 1.0).then_inc(picks, 1)
                pool.memset(pick_hh[r + 32 : r + 64, :], 1.0).then_inc(picks, 1)
            pool.wait_ge(ld_b, 16)
            pool.wait_ge(picks, 5)
            pool.tensor_scalar(brow_s[64:128, :], brow[64:128, :], WSCALE, None, ALU.mult).then_inc(brow_scaled, 1)
            pool.wait_ge(brow_scaled, 1)
            pool.wait_ge(hi_b, 1)
            pool.tensor_tensor(bsp[64:128, :], brow_s[64:128, :], bsp[64:128, :], ALU.subtract).then_inc(lo_b, 1)
            pool.wait_ge(ld_coup, 16)
            pool.wait_ge(lo_b, 1)
            pool.tensor_scalar(coup_s[:, :], coup[:, 1, :], WSCALE, None, ALU.mult).then_inc(coup_scaled, 1)
            pool.wait_ge(coup_scaled, 1)
            pool.wait_ge(hi_coup, 1)
            pool.tensor_tensor(cp2[:, 1, :], coup_s[:, :], cp1[:, 1, :], ALU.subtract).then_inc(lo_coup, 1)
            pool.wait_ge(g0_h1, 1)
            pool.tensor_tensor(h2[:, :], h[:, :], h1[:, :], ALU.subtract).then_inc(g0_h2, 1)

            def add_q0(i):
                step = outb[:, at(i - 2, W)]
                pool.tensor_tensor(step, step, q[0][:, :], ALU.add).then_inc(out_ready, 1)

            def body(i, before_last_gru=False, last_gru=False, last=False):
                first = isinstance(i, int) and i == 1
                if not (first or last_gru or last):
                    pool.tensor_tensor(xlo(i + 1), xs(i + 1), xhi(i + 1), ALU.subtract).then_inc(xlo_ready, 1)
                pool.tensor_tensor(outb[:, at(i - 1, W)], xs(i - 1), h[:, :], ALU.add).then_inc(xh_ready, 1)
                for s in (2, 3):
                    pool.wait_ge(sp0_ready[s], i)
                    if first and s == 2:
                        pool.wait_ge(g0_sdrive, 1)
                    pool.tensor_tensor(base[s][0][:, :], sp0[s][:, :], sdrive[:, :], ALU.add).then_inc(base_ready[s][0], 1)
                for s in (2, 3):
                    pool.wait_ge(base_ready[s][0], i)
                    pool.wait_ge(sq0_ready[s], i)
                    pool.tensor_tensor(base[s][1][:, :], sq0[s][:, :], base[s][0][:, :], ALU.add).then_inc(base_ready[s][1], 1)
                if last:
                    add_q0(i)
                    return
                pool.wait_ge(pq0_ready, i)
                pool.tensor_tensor(pacc[0][:, :], pacc0[:, :], pq0[:, :], ALU.add).then_inc(pacc_ready[0], 1)
                if not first:
                    add_q0(i)
                pool.wait_ge(n_ready, i)
                pool.tensor_tensor(dhn[:, :], h[:, :], n[:, :], ALU.subtract).then_inc(dhn_ready, 1)
                pool.wait_ge(dhn_ready, i)
                pool.wait_ge(z_ready, i)
                pool.tensor_tensor(zd[:, :], z[:, :], dhn[:, :], ALU.mult).then_inc(zd_ready, 1)
                pool.wait_ge(zd_ready, i)
                pool.tensor_tensor(h[:, :], n[:, :], zd[:, :], ALU.add).then_inc(h_ready, 1)
                pool.wait_ge(h_ready, i)
                pool.wait_ge(xb_ready, i)
                pool.tensor_tensor(drive[:, :], xb[:, :], h[:, :], ALU.add).then_inc(drive_ready, 1)
                if not last_gru:
                    pool.wait_ge(h1_ready, i)
                    pool.tensor_tensor(h2[:, :], h[:, :], h1[:, :], ALU.subtract).then_inc(h2_ready, 1)

            loop(pool, body)

        @block.tensor
        def _(pe):
            r_cols, z_cols, n_cols = 0, HALVES, 2 * HALVES

            def mm(ps, half, w, k, tile, mov, start):
                return pe.matmul(ps[:, half * B : (half + 1) * B], w[:, k, tile * P : (tile + 1) * P], mov,
                                 start=start, stop=True, skip_group_check=True)

            def bias(ps, first_tile, pick, start=True):
                for half in range(HALVES):
                    tile = first_tile + half
                    last = pe.matmul(ps[:, half * B : (half + 1) * B], bsp[:, tile * P : (tile + 1) * P], pick[:, :],
                                     start=start and half == 0, stop=True, skip_group_check=True)
                return last

            def x_products(ps, first_tile, t, ks=(0, 1), start=False):
                for half in range(HALVES):
                    tile = first_tile + half
                    for k in ks:
                        xk = [xhl[:, bass.ds(t * 2 * W + part * W + k * B, B)] for part in range(2)]
                        mm(ps, half, wih1, k, tile, xk[0], start and half == 0 and k == ks[0])
                        mm(ps, half, wih2, k, tile, xk[0], False)
                        last = mm(ps, half, wih1, k, tile, xk[1], False)
                return last

            def x_part(ps, first_tile, t, pick):
                bias(ps, first_tile, pick)
                return x_products(ps, first_tile, t)

            def h_part(ps, first_tile, parts=(1, 2), ks=(0, 1)):
                for part in parts:
                    for half in range(HALVES):
                        tile = first_tile + half
                        for k in ks:
                            if part == 1:
                                mm(ps, half, whh1, k, tile, h1[:, k * B : (k + 1) * B], False)
                                last = mm(ps, half, whh2, k, tile, h1[:, k * B : (k + 1) * B], False)
                            else:
                                last = mm(ps, half, whh1, k, tile, h2[:, k * B : (k + 1) * B], False)
                return last

            gates_of_x = ((ps_r, r_cols, pick_both), (ps_i, n_cols, pick_ih), (ps_z, z_cols, pick_both))
            pe.wait_ge(lo_x0, 1)
            for k in range(2):
                pe.wait_ge(lo_wih, k + 1)
                for ps, cols, _ in gates_of_x:
                    x_products(ps, cols, 0, ks=(k,), start=k == 0)
            pe.wait_ge(picks, 5)
            pe.wait_ge(lo_b, 1)
            for ps, cols, pick in gates_of_x:
                bias(ps, cols, pick, start=False)
            bias(ps_h, n_cols, pick_hh)
            for ps in (ps_first, ps_other):
                bias(ps, 0, pick_both).then_inc(ps_c_open, 1)
            pe.wait_ge(lo_h, 1)
            pe.wait_ge(lo_whh, 2)
            for ps, cols in ((ps_r, r_cols), (ps_h, n_cols), (ps_z, z_cols)):
                h_part(ps, cols, ks=(0,))
            for piece, (ps, cols, done) in enumerate(((ps_r, r_cols, g0_r), (ps_h, n_cols, g0_hn), (ps_z, z_cols, g0_z))):
                pe.wait_ge(lo_whh, 3 + piece)
                h_part(ps, cols, ks=(1,)).then_inc(done, 1)
            pe.wait_ge(g0_tr, 1)
            x_part(ps_r, r_cols, 1, pick_both)
            pe.wait_ge(g0_tz, 1)
            x_part(ps_z, z_cols, 1, pick_both)
            pe.wait_ge(g0_npre, 1)
            x_part(ps_i, n_cols, 1, pick_ih)
            bias(ps_h, n_cols, pick_hh)

            def fill_gap():
                for _ in range(2):
                    pe.matmul(ps_unread[:, 0:P], wih1[:, 0, 0:P], wih1[:, 0, 0:P], start=True, stop=True, skip_group_check=True)

            def coupling_hi(ps):
                for half in range(HALVES):
                    for k in range(2):
                        tk = t1[:, k * B : (k + 1) * B]
                        mm(ps, half, cp1, k, half, tk, False)
                        mm(ps, half, cp2, k, half, tk, False)

            def coupling_lo(ps):
                for half in range(HALVES):
                    for k in range(2):
                        last = mm(ps, half, cp1, k, half, t2[:, k * B : (k + 1) * B], False)
                return last

            pe.wait_ge(lo_coup, 2)

            def body(i, before_last_gru=False, last_gru=False, last=False):
                first = isinstance(i, int) and i == 1
                for s in range(4):
                    if s >= 2:
                        fill_gap()
                    pe.wait_ge(seed_ready[s], i)
                    pe.wait_ge(t_ready[s], i)
                    coupling_hi(ps_c[s])
                    pe.wait_ge(t2_ready[s], i)
                    coupling_lo(ps_c[s]).then_inc(c_ready[s], 1)
                    if last:
                        continue
                    if first and s == 0:
                        pe.wait_ge(g0_h2, 1)
                        h_part(ps_r, r_cols)
                        h_part(ps_h, n_cols).then_inc(rh_ready, 1)
                    if s == (1 if first else 0):
                        h_part(ps_z, z_cols).then_inc(zpre_ready, 1)
                        if not last_gru:
                            pe.wait_ge(tr_ready, i)
                            if not first:
                                pe.wait_ge(xlo_ready, i - 1)
                            x_part(ps_r, r_cols, i + 1, pick_both)
                    if last_gru:
                        continue
                    if s == 1:
                        pe.wait_ge(tz_ready, i)
                        x_part(ps_z, z_cols, i + 1, pick_both)
                    if s == 2:
                        pe.wait_ge(npre_ready, i)
                        x_part(ps_i, n_cols, i + 1, pick_ih)
                        bias(ps_h, n_cols, pick_hh)
                    if s == 3:
                        pe.wait_ge(h1_ready, i)
                        h_part(ps_r, r_cols, (1,))
                        h_part(ps_h, n_cols, (1,))
                        pe.wait_ge(h2_ready, i)
                        h_part(ps_r, r_cols, (2,))
                        h_part(ps_h, n_cols, (2,)).then_inc(rh_ready, 1)

            loop(pe, body)

        @block.scalar
        def _(act):
            def affine(out_, in_, scale, shift=0.0):
                return act.activation(out_, in_, ACT.Copy, scale=scale, bias=shift)

            def x_and_bias(t):
                for k in range(HALVES):
                    last = act.activation(xb[:, k * B : (k + 1) * B], x[:, bass.ds(t * W + k * B, B)], ACT.Identity,
                                          bias=fbias[:, k : k + 1])
                return last

            def tanh_and_square(s, i, point, ready, value):
                act.wait_ge(ready, value)
                act.activation(t[:, :], point[:, :], ACT.Tanh).then_inc(t_ready[s], 1)
                if s == 0:
                    act.wait_ge(q_ready[0], i)
                act.activation(sq[:, :], q[s][:, :], ACT.Square, scale=(STEP[s] / 3) ** 0.5).then_inc(sq_ready[s], 1)

            def shares_of_p0_and_q0(i):
                if isinstance(i, int) and i == 1:
                    act.wait_ge(g0_p0, 1)
                else:
                    act.wait_ge(p0_ready, i - 1)
                for s in (2, 3):
                    affine(sp0[s][:, :], p0[:, :], BASE_OF_P0[s], BASE_CONST[s]).then_inc(sp0_ready[s], 1)
                for s in (2, 3):
                    affine(sq0[s][:, :], q[0][:, :], BASE_OF_Q[s][0]).then_inc(sq0_ready[s], 1)

            act.wait_ge(picks, 1)
            act.activation(tr[:, 0:B], pick_both[:, :], ACT.Tanh).then_inc(tables, 1)

            act.wait_ge(ld_state, 16)
            affine(h1[:, :], h[:, :], 1.0).then_inc(hi_h, 1)
            act.wait_ge(ld_x0, 16)
            xv = x[:, 0 : XFIRST * W].rearrange("p (t w) -> p t w", w=W)
            xhlv = xhl[:, 0 : XFIRST * 2 * W].rearrange("p (t a w) -> p t a w", a=2, w=W)
            affine(xhlv[:, :, 0, :], xv, 1.0).then_inc(hi_x0, 1)
            tanh_and_square(0, 1, q[0], q_ready[0], 1)
            act.wait_ge(ld_b, 16)
            affine(bsp[:, :], brow[:, :], WSCALE).then_inc(hi_b, 1)
            for k in range(2):
                act.wait_ge(ld_wih[k], 16)
                affine(wih1[:, k, :], wih[:, k, :], WSCALE).then_inc(hi_wih, 1)
                if k == 0:
                    act.wait_ge(ld_fb, 16)
                    x_and_bias(0).then_inc(g0_xb, 1)
            for k, cols in whh_pieces:
                act.wait_ge(ld_whh[k], 16)
                affine(whh1[:, k, cols], whh[:, k, cols], WSCALE).then_inc(hi_whh, 1)
            act.wait_ge(ld_coup, 16)
            affine(cp1[:, :, :], coup[:, :, :], WSCALE).then_inc(hi_coup, 1)

            act.wait_ge(g0_r, 1)
            act.activation(tr[:, :], ps_r[:, 0:W], ACT.Tanh, scale=0.5 / WSCALE).then_inc(g0_tr, 1)
            act.wait_ge(g0_z, 1)
            act.activation(tz[:, :], ps_z[:, 0:W], ACT.Tanh, scale=0.5 / WSCALE).then_inc(g0_tz, 1)
            act.wait_ge(g0_tz, 1)
            affine(z[:, :], tz[:, :], 0.5, 0.5).then_inc(g0_zs, 1)
            act.wait_ge(g0_npre, 1)
            act.activation(n[:, :], npre[:, :], ACT.Tanh, scale=1.0 / WSCALE).then_inc(g0_n, 1)
            affine(omz[:, :], tz[:, :], -0.5, 0.5).then_inc(g0_n, 1)
            shares_of_p0_and_q0(1)
            act.wait_ge(g0_drive, 1)
            affine(sdrive1[:, :], drive[:, :], WSCALE, BASE_CONST[1]).then_inc(g0_sdrive1, 1)
            act.wait_ge(g0_h, 1)
            affine(h1[:, :], h[:, :], 1.0).then_inc(g0_h1, 1)
            affine(sdrive[:, :], drive[:, :], WSCALE).then_inc(g0_sdrive, 1)

            def body(i, before_last_gru=False, last_gru=False, last=False):
                first = isinstance(i, int) and i == 1
                for s in range(4):
                    if s > 0:
                        tanh_and_square(s, i, q[s], q_ready[s], i)
                    elif not first:
                        tanh_and_square(0, i, qraw, qraw_ready, i - 1)
                    if s == (1 if first else 0) and not last:
                        act.wait_ge(rh_ready, i)
                        act.activation(tr[:, :], ps_r[:, 0:W], ACT.Tanh, scale=0.5 / WSCALE).then_inc(tr_ready, 1)
                    if s == 0 and not first:
                        shares_of_p0_and_q0(i)
                    if last:
                        continue
                    if s == 1:
                        affine(pacc0[:, :], p0[:, :], P_OF_P0, P_CONST)
                        affine(pq0[:, :], q[0][:, :], P_OF_Q[0]).then_inc(pq0_ready, 1)
                        act.wait_ge(zpre_ready, i)
                        act.activation(tz[:, :], ps_z[:, 0:W], ACT.Tanh, scale=0.5 / WSCALE).then_inc(tz_ready, 1)
                        act.wait_ge(tz_ready, i)
                        affine(z[:, :], tz[:, :], 0.5, 0.5).then_inc(z_ready, 1)
                        act.wait_ge(npre_ready, i)
                        act.activation(n[:, :], npre[:, :], ACT.Tanh, scale=1.0 / WSCALE).then_inc(n_ready, 1)
                    if s == 2:
                        if first:
                            act.wait_ge(ld_x, 16)
                        if not (before_last_gru or last_gru):
                            affine(xhi(i + 2), xs(i + 2), 1.0)
                        x_and_bias(i).then_inc(xb_ready, 1)
                    if s == 3:
                        if not last_gru:
                            act.wait_ge(h_ready, i)
                            affine(h1[:, :], h[:, :], 1.0).then_inc(h1_ready, 1)
                        act.wait_ge(drive_ready, i)
                        affine(sdrive[:, :], drive[:, :], WSCALE).then_inc(sdrive_ready, 1)
                        affine(sdrive1[:, :], drive[:, :], WSCALE, BASE_CONST[1]).then_inc(sdrive1_ready, 1)

            loop(act, body)

        @block.vector
        def _(dve):
            def stt(out_, in0, scalar, in1, op0=ALU.mult, op1=ALU.add):
                return dve.scalar_tensor_tensor(out_, in0, scalar, in1, op0, op1)

            def clip(out_, in_):
                return dve.tensor_scalar(out_, in_, CLAMP, -CLAMP, ALU.min, ALU.max)

            def seed_0():
                return stt(ps_c[0][:, 0:W], p0[:, :], BASE_OF_P0[0], sdrive[:, :])

            def tanh_rest(s, i):
                dve.wait_ge(t_ready[s], i)
                dve.tensor_tensor(t2[:, :], t[:, :], t1, ALU.subtract).then_inc(t2_ready[s], 1)

            def cube(s, i):
                dve.wait_ge(sq_ready[s], i)
                dve.wait_ge(q_ready[s], i)
                stt(cub[:, :], sq[:, :], SELF[s], q[s][:, :], ALU.subtract, ALU.mult).then_inc(cub_ready[s], 1)

            dve.wait_ge(ld_state, 16)
            dve.tensor_copy(q[0][:, :], h[:, :]).then_inc(q_ready[0], 1)
            dve.tensor_copy(p0[:, :], h[:, :]).then_inc(g0_p0, 1)

            dve.wait_ge(hi_h, 1)
            dve.tensor_tensor(h2[:, :], h[:, :], h1[:, :], ALU.subtract).then_inc(lo_h, 1)
            dve.wait_ge(hi_x0, 1)
            xv = x[:, 0 : XFIRST * W].rearrange("p (t w) -> p t w", w=W)
            xhlv = xhl[:, 0 : XFIRST * 2 * W].rearrange("p (t a w) -> p t a w", a=2, w=W)
            dve.tensor_tensor(xhlv[:, :, 1, :], xv, xhlv[:, :, 0, :], ALU.subtract).then_inc(lo_x0, 1)
            dve.tensor_scalar(p0_part[:, :], h[:, :], BASE_OF_P0[0], None, ALU.mult).then_inc(p0_part_ready, 1)
            tanh_rest(0, 1)
            cube(0, 1)
            for k in range(2):
                dve.wait_ge(hi_wih, k + 1)
                stt(wih2[:, k, :], wih[:, k, :], WSCALE, wih1[:, k, :], op1=ALU.subtract).then_inc(lo_wih, 1)
            for piece, (k, cols) in enumerate(whh_pieces):
                dve.wait_ge(hi_whh, piece + 1)
                stt(whh2[:, k, cols], whh[:, k, cols], WSCALE, whh1[:, k, cols], op1=ALU.subtract).then_inc(lo_whh, 1)

            dve.wait_ge(g0_tr, 1)
            dve.wait_ge(g0_hn, 1)
            stt(rh[:, :], tr[:, :], 1.0, ps_h[:, 0:W], ALU.add, ALU.mult).then_inc(g0_rh, 1)
            dve.wait_ge(g0_rh, 1)
            stt(npre[:, :], rh[:, :], 0.5, ps_i[:, 0:W]).then_inc(g0_npre, 1)
            dve.wait_ge(hi_coup, 1)
            stt(cp2[:, 0, :], coup[:, 0, :], WSCALE, cp1[:, 0, :], op1=ALU.subtract).then_inc(lo_coup, 1)
            dve.wait_ge(g0_zs, 1)
            dve.tensor_tensor(zh[:, :], z[:, :], h[:, :], ALU.mult).then_inc(g0_zh, 1)
            dve.wait_ge(g0_xb, 1)
            dve.wait_ge(g0_zh, 1)
            dve.tensor_tensor(xbzh[:, :], xb[:, :], zh[:, :], ALU.add).then_inc(g0_xbzh, 1)
            dve.wait_ge(g0_n, 2)
            dve.tensor_tensor(nz[:, :], n[:, :], omz[:, :], ALU.mult).then_inc(g0_nz, 1)
            dve.wait_ge(g0_nz, 1)
            dve.wait_ge(g0_xbzh, 1)
            dve.tensor_tensor(drive[:, :], nz[:, :], xbzh[:, :], ALU.add).then_inc(g0_drive, 1)
            dve.tensor_tensor(h[:, :], nz[:, :], zh[:, :], ALU.add).then_inc(g0_h, 1)
            dve.wait_ge(g0_drive, 1)
            dve.wait_ge(p0_part_ready, 1)
            dve.wait_ge(ps_c_open, 2)
            stt(ps_first[:, 0:W], drive[:, :], WSCALE, p0_part[:, :]).then_inc(seed_ready[0], 1)

            def base_term(s, r, i):
                dve.wait_ge(base_ready[s][r], i)
                return stt(base[s][r + 1][:, :], q[r][:, :], BASE_OF_Q[s][r], base[s][r][:, :]).then_inc(base_ready[s][r + 1], 1)

            def advance(s, i, dst, dst_ready):
                dve.wait_ge(c_ready[s], i)
                dve.wait_ge(cub_ready[s], i)
                stt(dst[:, :], ps_c[s][:, 0:W], STEP[s] / WSCALE, cub[:, :], op1=ALU.subtract).then_inc(dst_ready, 1)

            def seed(s, i):
                dve.wait_ge(q_ready[s], i)
                dve.wait_ge(base_ready[s][s], i)
                stt(ps_c[s][:, 0:W], q[s][:, :], -SHIFT[s] * UNIT[s], base[s][s][:, :]).then_inc(seed_ready[s], 1)

            def body(i, before_last_gru=False, last_gru=False, last=False):
                first = isinstance(i, int) and i == 1
                if not first:
                    dve.wait_ge(qraw_ready, i - 1)
                    clip(q[0][:, :], qraw[:, :]).then_inc(q_ready[0], 1)
                    dve.wait_ge(sdrive1_ready, i - 1)
                else:
                    dve.wait_ge(g0_sdrive1, 1)
                stt(base[1][0][:, :], p0[:, :], BASE_OF_P0[1], sdrive1[:, :]).then_inc(base_ready[1][0], 1)
                if not first:
                    tanh_rest(0, i)
                    cube(0, i)
                base_term(1, 0, i)
                advance(0, i, q[1], q_ready[1])

                def twice_r_hn():
                    dve.wait_ge(tr_ready, i)
                    stt(rh[:, :], tr[:, :], 1.0, ps_h[:, 0:W], ALU.add, ALU.mult).then_inc(m_ready, 1)

                def gru_candidate():
                    dve.wait_ge(m_ready, i)
                    stt(npre[:, :], rh[:, :], 0.5, ps_i[:, 0:W]).then_inc(npre_ready, 1)

                if not (first or last):
                    twice_r_hn()
                seed(1, i)
                if not (first or last):
                    gru_candidate()
                tanh_rest(1, i)
                cube(1, i)
                base_term(2, 1, i)
                if first:
                    twice_r_hn()
                    gru_candidate()
                advance(1, i, q[2], q_ready[2])

                base_term(3, 1, i)
                seed(2, i)
                base_term(3, 2, i)
                tanh_rest(2, i)
                cube(2, i)
                if not last:
                    dve.wait_ge(pacc_ready[0], i)
                    stt(pacc[1][:, :], q[1][:, :], P_OF_Q[1], pacc[0][:, :]).then_inc(pacc_ready[1], 1)
                advance(2, i, q[3], q_ready[3])

                if not last:
                    dve.wait_ge(pacc_ready[1], i)
                    stt(pacc[2][:, :], q[2][:, :], P_OF_Q[2], pacc[1][:, :]).then_inc(pacc_ready[2], 1)
                seed(3, i)
                if not last:
                    dve.wait_ge(pacc_ready[2], i)
                    stt(praw[:, :], q[3][:, :], P_OF_Q[3], pacc[2][:, :]).then_inc(praw_ready, 1)
                tanh_rest(3, i)
                cube(3, i)
                if not last:
                    dve.wait_ge(praw_ready, i)
                    clip(p0[:, :], praw[:, :]).then_inc(p0_ready, 1)
                advance(3, i, qraw, qraw_ready)
                if not last:
                    dve.wait_ge(sdrive_ready, i)
                    dve.wait_ge(p0_ready, i)
                    seed_0().then_inc(seed_ready[0], 1)

            loop(dve, body)
            dve.wait_ge(qraw_ready, T)
            dve.wait_ge(out_ready, T - 1)
            clip(q[0][:, :], qraw[:, :]).then_inc(q_ready[0], 1)
            dve.wait_ge(q_ready[0], T + 1)
            dve.wait_ge(xh_ready, T)
            dve.tensor_tensor(outb[:, at(T - 1, W)], outb[:, at(T - 1, W)], q[0][:, :], ALU.add).then_inc(out_ready, 1)


def kernel(x, cond_2048, L0_cond_W_ih, L0_cond_W_hh, L0_cond_b_ih, L0_cond_b_hh, L1_cond_coupling, L1_cond_bias):
    import concourse.bacc as bacc
    import numpy as np
    from concourse.bass_utils import run_bass_kernel_spmd

    def features_first(a):
        a = np.asarray(a)
        return np.ascontiguousarray(np.moveaxis(a.reshape(HALVES, P, *a.shape[1:]), 0, 1))

    x, cond = np.asarray(x), np.asarray(cond_2048)
    nb, T, D = x.shape
    xt = features_first(x.transpose(2, 1, 0))
    arrays = {
        "x": np.ascontiguousarray(xt.transpose(0, 2, 1, 3)).reshape(P, T, W),
        "cond": features_first(cond.T).reshape(P, W),
        "wih": features_first(L0_cond_W_ih),
        "whh": features_first(L0_cond_W_hh),
        "biases": np.stack([L0_cond_b_ih, L0_cond_b_hh] * 2),
        "coup": features_first(np.asarray(L1_cond_coupling).T),
        "fbias": features_first(L1_cond_bias).reshape(P, HALVES),
    }
    nc = bacc.Bacc("TRN2", target_bir_lowering=False, num_devices=1)
    args = [nc.dram_tensor(k + "_dram", a.shape, mybir.dt.from_np(a.dtype), kind="ExternalInput").ap() for k, a in arrays.items()]
    out = nc.dram_tensor("out_dram", (T, P, W), mybir.dt.from_np(np.dtype("float32")), kind="ExternalOutput").ap()
    build(nc, *args, out)
    got = run_bass_kernel_spmd(nc, [{k + "_dram": a for k, a in arrays.items()}], core_ids=[0]).results[0]["out_dram"]
    return np.ascontiguousarray(np.asarray(got).reshape(T, P, HALVES, nb).transpose(3, 0, 2, 1)).reshape(nb, T, D)
```
